# Optimizing a Trainium2 kernel written in Bass

```python
import numpy as np
import jax
import jax.numpy as jnp

def _softmax(x, axis=-1):
    return jax.nn.softmax(x, axis=axis)

def _gelu(x):
    return jax.nn.gelu(x, approximate=True)

def _silu(x):
    return jax.nn.silu(x)

def _sigmoid(x):
    return jax.nn.sigmoid(x)

def _layernorm(x, axis=-1, eps=1e-05):
    m = jnp.mean(x, axis=axis, keepdims=True)
    v = jnp.var(x, axis=axis, keepdims=True)
    return (x - m) / jnp.sqrt(v + eps)

def _scatter_add(tgt, idx, src, axis=0):
    return tgt.at[idx].add(src)

def _segment_sum(src, seg, n):
    return jax.ops.segment_sum(src, seg, n)
kernel_name = 'mk_adj_preln_d2_adj_r2_c98047'

def setup_inputs(seed: int=0):
    np.random.seed(seed)
    _w = jnp.asarray

    def _rec_inputs():
        import jax
        import jax.numpy as jnp
        _gk = jax.random.key(seed)
        x = -0.0005207 + 1.001 * jax.random.normal(jax.random.fold_in(_gk, 1), (8, 1024, 128), jnp.float32)
        _a = jax.random.bernoulli(jax.random.fold_in(_gk, 2), 0.00390625, (1024, 1024))
        _a = jnp.logical_or(_a, jnp.swapaxes(_a, -1, -2))
        _a = jnp.logical_or(_a, jnp.eye(1024, dtype=bool))
        adj = _a.astype(jnp.int32)
        return (x, adj)
    x, adj = _rec_inputs()

    def _L0_gnn_setup():
        import jax, jax.numpy as jnp
        import numpy as np
        import math
        CHUNK = 128
        NUM_HEADS = 4
        EPS = 1e-05
        key = jax.random.key(seed)
        ks = jax.random.split(key, 12)
        B, N, F = (4, 1024, 128)
        x = jax.random.normal(ks[0], (B, N, F), dtype=jnp.float32)
        adj_matrix = jax.random.randint(ks[1], (N, N), 0, 2, dtype=jnp.int32)
        s = 1.0 / math.sqrt(F)
        Wq = jax.random.normal(ks[2], (F, F), dtype=jnp.float32) * s
        bq = jnp.zeros((F,), dtype=jnp.float32)
        Wk = jax.random.normal(ks[3], (F, F), dtype=jnp.float32) * s
        bk = jnp.zeros((F,), dtype=jnp.float32)
        Wv = jax.random.normal(ks[4], (F, F), dtype=jnp.float32) * s
        bv = jnp.zeros((F,), dtype=jnp.float32)
        Wo = jax.random.normal(ks[5], (F, F), dtype=jnp.float32) * s
        bo = jnp.zeros((F,), dtype=jnp.float32)
        gamma = jnp.ones((F,), dtype=jnp.float32)
        beta = jnp.zeros((F,), dtype=jnp.float32)
        return {'x': x, 'adj_matrix': adj_matrix, 'Wq': Wq, 'bq': bq, 'Wk': Wk, 'bk': bk, 'Wv': Wv, 'bv': bv, 'Wo': Wo, 'bo': bo, 'gamma': gamma, 'beta': beta}
    _L0_gnn_all = _L0_gnn_setup()
    _L0_gnn_in = {k: v for k, v in _L0_gnn_all.items() if k in ('Wq', 'bq', 'Wk', 'bk', 'Wv', 'bv', 'Wo', 'bo', 'gamma', 'beta')}
    del _L0_gnn_all

    def _L1_gnn_setup():
        import jax, jax.numpy as jnp
        import numpy as np
        LEAKY_ALPHA = 0.2
        key = jax.random.key(seed)
        k1, k2, k3, k4 = jax.random.split(key, 4)
        B, N, Fin, Fout = (8, 1024, 128, 128)
        h = jax.random.normal(k1, (B, N, Fin), dtype=jnp.float32)
        adj = jax.random.randint(k2, (N, N), 0, 2, dtype=jnp.int32)
        W = jax.random.normal(k3, (Fin, Fout), dtype=jnp.float32) * (1.414 * (6.0 / (Fin + Fout)) ** 0.5)
        a = jax.random.normal(k4, (2 * Fout, 1), dtype=jnp.float32) * (1.414 * (6.0 / (2 * Fout + 1)) ** 0.5)
        return {'h': h, 'adj': adj, 'W': W, 'a': a}
    _L1_gnn_all = _L1_gnn_setup()
    _L1_gnn_in = {k: v for k, v in _L1_gnn_all.items() if k in ('W', 'a')}
    del _L1_gnn_all
    return {'x': x, 'adj': adj, 'L0_gnn_Wq': _L0_gnn_in['Wq'], 'L0_gnn_bq': _L0_gnn_in['bq'], 'L0_gnn_Wk': _L0_gnn_in['Wk'], 'L0_gnn_bk': _L0_gnn_in['bk'], 'L0_gnn_Wv': _L0_gnn_in['Wv'], 'L0_gnn_bv': _L0_gnn_in['bv'], 'L0_gnn_Wo': _L0_gnn_in['Wo'], 'L0_gnn_bo': _L0_gnn_in['bo'], 'L0_gnn_gamma': _L0_gnn_in['gamma'], 'L0_gnn_beta': _L0_gnn_in['beta'], 'L1_gnn_W': _L1_gnn_in['W'], 'L1_gnn_a': _L1_gnn_in['a']}

def reference(x, adj, L0_gnn_Wq, L0_gnn_bq, L0_gnn_Wk, L0_gnn_bk, L0_gnn_Wv, L0_gnn_bv, L0_gnn_Wo, L0_gnn_bo, L0_gnn_gamma, L0_gnn_beta, L1_gnn_W, L1_gnn_a):
    import jax
    import jax.numpy as jnp

    def _L0_gnn_ref(x, adj_matrix, Wq, bq, Wk, bk, Wv, bv, Wo, bo, gamma, beta):
        import jax, jax.numpy as jnp
        import numpy as np
        import math
        CHUNK = 128
        NUM_HEADS = 4
        EPS = 1e-05
        B, N, Fin = x.shape
        H = NUM_HEADS
        Dout = Wq.shape[0]
        Dh = Dout // H
        Nc = N // CHUNK
        q = (x @ Wq.T + bq).reshape(B, N, H, Dh).transpose(0, 2, 1, 3)
        k = (x @ Wk.T + bk).reshape(B, N, H, Dh).transpose(0, 2, 1, 3)
        v = (x @ Wv.T + bv).reshape(B, N, H, Dh).transpose(0, 2, 1, 3)
        kc = k.reshape(B, H, Nc, CHUNK, Dh)
        vc = v.reshape(B, H, Nc, CHUNK, Dh)
        scores = jnp.einsum('bhnd,bhjcd->bhnjc', q, kc) / jnp.sqrt(jnp.asarray(Dh, dtype=q.dtype))
        scores = jnp.clip(scores, -10.0, 10.0)
        mask = adj_matrix.reshape(N, Nc, CHUNK)[None, None]
        scores = jnp.where(mask == 0, jnp.asarray(-10.0, scores.dtype), scores)
        attn = jax.nn.softmax(scores, axis=-1)
        ctx = jnp.einsum('bhnjc,bhjcd->bhnd', attn, vc)
        ctx = ctx.transpose(0, 2, 1, 3).reshape(B, N, Dout)
        out = ctx @ Wo.T + bo
        out = out + x
        mu = jnp.mean(out, axis=-1, keepdims=True)
        var = jnp.mean(jnp.square(out - mu), axis=-1, keepdims=True)
        out = (out - mu) * jax.lax.rsqrt(var + EPS) * gamma + beta
        return out

    def _L1_gnn_ref(h, adj, W, a):
        import jax, jax.numpy as jnp
        import numpy as np
        LEAKY_ALPHA = 0.2
        Fout = W.shape[1]
        Wh = jnp.einsum('bnf,fo->bno', h, W)
        a1 = a[:Fout, 0]
        a2 = a[Fout:, 0]
        s_i = Wh @ a1
        s_j = Wh @ a2
        e = jax.nn.leaky_relu(s_i[:, :, None] + s_j[:, None, :], negative_slope=LEAKY_ALPHA)
        N = Wh.shape[1]
        mask = (adj > 0) | jnp.eye(N, dtype=bool)
        e = jnp.where(mask[None, :, :], e, -jnp.inf)
        attention = jax.nn.softmax(e, axis=-1)
        attention = jnp.nan_to_num(attention, nan=0.0)
        h_prime = jnp.einsum('bij,bjo->bio', attention, Wh)
        return jax.nn.elu(h_prime)
    h = jnp.maximum(_layernorm(x, axis=-1), 0.0)
    x = x + _L0_gnn_ref(h, adj, L0_gnn_Wq, L0_gnn_bq, L0_gnn_Wk, L0_gnn_bk, L0_gnn_Wv, L0_gnn_bv, L0_gnn_Wo, L0_gnn_bo, L0_gnn_gamma, L0_gnn_beta)
    h = jnp.maximum(_layernorm(x, axis=-1), 0.0)
    x = x + _L1_gnn_ref(h, adj, L1_gnn_W, L1_gnn_a)
    return x

_drawn_inputs = setup_inputs


def setup_inputs(seed=0):
    import zlib

    import numpy as np

    out = dict(_drawn_inputs(seed))
    spreads = {'L0_gnn_bq': (0.0, 0.8),
     'L0_gnn_bk': (0.0, 2.0),
     'L0_gnn_bv': (0.0, 0.1),
     'L0_gnn_bo': (0.0, 0.399),
     'L0_gnn_gamma': (1.0, 0.2),
     'L0_gnn_beta': (0.0, 0.1)}
    factors = {}
    for name, (base, spread) in spreads.items():
        noise = np.random.default_rng([zlib.crc32(name.encode()), seed]).standard_normal(out[name].shape)
        drawn = base * np.exp(spread * noise) if base else spread * noise
        out[name] = jnp.asarray(drawn.astype(out[name].dtype))
    for name, factor in factors.items():
        out[name] = (out[name] * factor).astype(out[name].dtype)
    return out
```

```python
from contextlib import ExitStack

import concourse.bass as bass
from concourse import mybir

F32 = mybir.dt.float32
F32R = mybir.dt.float32r
BF16 = mybir.dt.bfloat16
I32 = mybir.dt.int32
ALU = mybir.AluOpType
ACT = mybir.ActivationFunctionType

P = 128
BATCHES, N, D = 8, 1024, 128
HEADS = 4
DH = D // HEADS
CHUNKS = N // P
HALF = N // 2
TILES = HALF // P
STEPS = 2 * CHUNKS
EPS = 1e-5
LOW, HIGH = 4.5399929762484854e-05, 22026.465794806718
OUT_OF_SIGHT = -1e30
SLOPE = 0.2
RING = 12
PEAK_STEPS = CHUNKS + 3
TURN, SUMS, OUT_A, OUT_B = 4, 5, 6, 7

JOBS = sorted(
    [(q, c, 1, f"gather{q}{c - 1}", q - 1) for q in (0, 1) for c in range(1, CHUNKS)]
    + [(q, 0, 0, f"gather_last{q}", -1) for q in (0, 1)]
    + [(q, 0, 3, f"turn_sums{q}", q - 1) for q in (0, 1)]
    + [(q, 1, 0, f"turn_context{q}", -1) for q in (0, 1)]
    + [(q, 2, 3, f"project{q}", -1) for q in (0, 1)]
    + [(q, 7, 3, f"turn_hidden{q}", -1) for q in (0, 1)]
    + [
        (0, 0, 2, "to_row0", -2), (0, 3, 3, "to_row1", -2),
        (0, 1, 2, "gat_sums1", -3), (0, 2, 0, "gat_turn_sums1", -3), (0, 3, 2, "gat_turn1", -3),
        (0, 2, 2, "query1", 0), (0, 3, 0, "value1", 0),
        (0, 4, 0, "ends", -2), (0, 4, 2, "wh0", -2), (0, 5, 0, "wh1", -2),
        (0, 5, 2, "from_row0", -2), (0, 6, 0, "from_row1", -2),
        (0, 4, 3, "turn_x0", 1), (0, 5, 3, "turn_x1", 1),
        (0, 7, 0, "peak_row0", -2), (0, 7, 2, "peak_row1", -2),
        (1, 1, 2, "query0", 1), (1, 2, 2, "key0", 1), (1, 5, 3, "value0", 1), (1, 6, 2, "key1", 1),
        (1, 5, 0, "gat_sums0", -2), (1, 5, 2, "gat_turn_sums0", -2), (1, 6, 0, "gat_turn0", -2),
    ]
)
JOB_AT = {(q, c, j): (name, off) for q, c, j, name, off in JOBS}
ORDER = {name: n for n, (_, _, _, name, _) in enumerate(JOBS)}
OFFSET = {name: off for _, _, _, name, off in JOBS}
FIRST, LAST = -1, BATCHES + 2
LOOP = range(3, BATCHES - 2)


class Graph:

    def __init__(self, offset, register=None):
        self.offset, self.register = offset, register

    def __add__(self, n):
        return Graph(self.offset + n, self.register)

    def live(self):
        return self.register is not None or 0 <= self.offset < BATCHES

    def times(self, k, plus=0):
        constant = self.offset * k + plus
        return constant if self.register is None else self.register * k + constant


def jobs_of(i):
    return [n for n, (_, _, _, _, off) in enumerate(JOBS) if 0 <= i + off < BATCHES]


def jobs_before(i):
    return sum(len(jobs_of(k)) for k in range(FIRST, i))


def count(name, i):
    n = ORDER[name]
    if i.register is None:
        return jobs_before(i.offset) + sum(m <= n for m in jobs_of(i.offset))
    if i.offset < 0:
        missing = set(range(len(JOBS))) - set(jobs_of(LOOP[0] - 1))
        assert i.offset == -1 and all(m < n for m in missing), name
    at = Graph(i.offset - LOOP[0], i.register)
    return at.times(len(JOBS), jobs_before(LOOP[0]) + n + 1)


def iterations(engine, body):
    for i in range(FIRST, LOOP[0]):
        body(Graph(i))
    with engine.Fori(LOOP[0], LOOP[-1] + 1) as register:
        body(Graph(0, register))
    for i in range(LOOP[-1] + 1, LAST + 1):
        body(Graph(i))


def next_step(i, q, c):
    return (i, q, c + 1) if c + 1 < CHUNKS else (i, 1, 0) if q == 0 else (i + 1, 0, 0)


def last_step(i, q, c):
    return (i, q, c - 1) if c else (i, 0, CHUNKS - 1) if q else (i + -1, 1, CHUNKS - 1)


def slot(step, h, plus=0):
    i, q, c = step
    return i.times(STEPS * HEADS, (q * CHUNKS + c) * HEADS + h + plus)


def number(step, plus=0):
    i, q, c = step
    return i.times(STEPS, q * CHUNKS + c + plus)


def build(nc, x, adj, Wq, bq, Wk, bk, Wv, bv, Wo, bo, gamma, beta, W, a, out):
    x_half = x.rearrange("b (h t p) f -> (b h) p t f", h=2, p=P)
    out_half = out.rearrange("b (h t p) f -> (b h) p t f", h=2, p=P)
    adj_tile = adj.rearrange("(t p) j -> t p j", p=P)
    h_kept = nc.dram_tensor("h_kept", (2 * BATCHES, P, TILES, D), F32, kind="Internal").ap()
    x1_kept = nc.dram_tensor("x1_kept", (2 * BATCHES, P, TILES, D), F32, kind="Internal").ap()

    ctx = ExitStack()
    with ctx:

        def sb(name, shape, dt=F32):
            return ctx.enter_context(nc.sbuf_tensor(name, shape, dt))

        def pb(name, shape, dt=F32):
            return ctx.enter_context(nc.psum_tensor(name, shape, dt))

        def sem(name):
            return ctx.enter_context(nc.semaphore(name))

        cap = sb("cap", [P, CHUNKS, N])
        see_t = sb("see_t", [P, CHUNKS, N], BF16)
        see = sb("see", [P, CHUNKS, N], BF16)
        key_stack = sb("key_stack", [P, HEADS, N], F32R)
        query_stack = sb("query_stack", [P, HEADS, N], F32R)
        key_parts = sb("key_parts", [P, 2, HALF], F32R)
        query_parts = sb("query_parts", [P, 2, HALF], F32R)
        value = sb("value", [P, CHUNKS, D])
        probs = sb("probs", [P, 2, HEADS, HALF])
        context = sb("context", [P, CHUNKS, HALF])
        sums = sb("sums", [P, HALF])
        inverse = sb("inverse", [P, TILES, HEADS, CHUNKS])
        gathered = sb("gathered", [P, TILES, D])
        scaled = sb("scaled", [P, TILES, D])
        context_t = sb("context_t", [P, HALF])
        x_in = sb("x_in", [P, 2, TILES, D])
        h_t = sb("h_t", [P, N])
        res = sb("res", [P, TILES, D])
        h1 = sb("h1", [P, TILES, D])
        h1_t = sb("h1_t", [P, N])
        wh = sb("wh", [P, CHUNKS, D])
        from_row = sb("from_row", [P, N])
        to_row = sb("to_row", [P, N])
        ends = sb("ends", [P, CHUNKS, 4])
        peak = sb("peak", [P, CHUNKS])
        row_shift = sb("row_shift", [P, CHUNKS])
        gat_inverse = sb("gat_inverse", [P, TILES])
        ring = sb("ring", [P, RING, HALF])
        w_in = h_t[:, 0:4 * D].rearrange("p (n f) -> p n f", n=4)
        w_t = sb("w_t", [P, 4, D])
        w1 = sb("w1", [P, D])
        a_in = sb("a_in", [P, 2])
        w1_a = sb("w1_a", [P, 4])
        bias_col = sb("bias_col", [P, 2])
        rows = sb("rows", [P, 4, D])
        eye = sb("eye", [P, P])
        eye_b = ring[:, 3, 0:P // 2].bitcast(BF16)
        not_eye = ring[:, 2, 0:P // 2].bitcast(BF16)
        one_of = sb("one_of", [P, CHUNKS, DH])
        ones = sb("ones", [P, DH])
        pick = sb("pick", [P, 1])
        eps = sb("eps", [P, TILES])
        minus_half = sb("minus_half", [P, TILES])
        small = sb("small", [P, 4, TILES * 11])
        norm = {}
        for n, s in enumerate(("x0", "x1", "y", "z")):
            norm[s] = (small[:, n, 0:24].rearrange("p (t k) -> p t k", t=TILES),
                       small[:, n, 24:32].rearrange("p (t k) -> p t k", t=TILES),
                       small[:, n, 32:36], small[:, n, 36:40], small[:, n, 40:44])

        score = pb("score", [P, HEADS, HALF])
        ctx_ps = pb("ctx_ps", [P, HALF])
        sum_ps = pb("sum_ps", [P, HALF])
        work = pb("work", [P, HALF])
        gat_ps = pb("gat_ps", [P, HALF])
        work_tiles = work[:, :].rearrange("p (t f) -> p t f", t=TILES)

        w_loaded = sem("w_loaded")
        adj_loaded = [sem(f"adj_loaded{t}") for t in range(CHUNKS)]
        x_loaded = sem("x_loaded")
        h_stored = sem("h_stored")
        res_loaded = sem("res_loaded")
        x1_stored = sem("x1_stored")
        x1_loaded = sem("x1_loaded")
        out_stored = sem("out_stored")
        keys_stacked = sem("keys_stacked")
        queries_stacked = sem("queries_stacked")
        consts_made = sem("consts_made")
        consts_step = sem("consts_step")
        adj_cast = sem("adj_cast")
        adj_turned = sem("adj_turned")
        adj_used = sem("adj_used")
        masks_step = sem("masks_step")
        w_turned = sem("w_turned")
        w_ready = sem("w_ready")
        passed = sem("passed")
        scores_done = sem("scores_done")
        exp_done = sem("exp_done")
        probs_ready = sem("probs_ready")
        context_done = sem("context_done")
        context_read = sem("context_read")
        sums_done = sem("sums_done")
        sums_read = sem("sums_read")
        work_done = sem("work_done")
        work_read = sem("work_read")
        high_ready = sem("high_ready")
        gathered_step = sem("gathered_step")
        res_ready = sem("res_ready")
        y_summed = sem("y_summed")
        gamma_done = sem("gamma_done")
        x1_ready = sem("x1_ready")
        stats_done = {s: sem(f"{s}_stats_done") for s in norm}
        moments_done = {s: sem(f"{s}_moments_done") for s in norm}
        spread_done = {s: sem(f"{s}_spread_done") for s in norm}
        rstd_done = {s: sem(f"{s}_rstd_done") for s in norm}
        shift_done = {s: sem(f"{s}_shift_done") for s in norm}
        normed = {s: sem(f"{s}_normed") for s in norm}
        peak_step = sem("peak_step")
        peak_done = sem("peak_done")
        leaky_done = sem("leaky_done")
        hidden_done = sem("hidden_done")
        shifted_done = sem("shifted_done")
        gat_exp_done = sem("gat_exp_done")
        gat_done = sem("gat_done")
        gat_read = sem("gat_read")
        divided = sem("divided")
        negative_ready = sem("negative_ready")
        negative_exp = sem("negative_exp")
        elu_step = sem("elu_step")
        out_ready = sem("out_ready")

        def wait(engine, semaphore, value):
            if not isinstance(value, int) or value > 0:
                engine.wait_ge(semaphore, value)

        def stand_alone(engine):
            engine.sem_inc(passed, 1)

        def adj_raw(t):
            home = context if t < 4 else probs[:, 0] if t < 6 else probs[:, 1]
            at = t if t < 4 else (t - 4) % 2
            return home[:, 2 * at:2 * at + 2, :].rearrange("p a n -> p (a n)").bitcast(I32)

        def adj_bf16(t):
            return ring[:, t % 2, :].bitcast(BF16)

        def adj_turned_ps(t):
            return score[:, t % 4, :].bitcast(BF16).rearrange("p (j i) -> p j i", i=P)

        def ring_tiles(s):
            return ring[:, s, :].rearrange("p (t f) -> p t f", t=TILES)

        block = ctx.enter_context(nc.Block())

        @block.sync
        def _(sp):
            for t in range(CHUNKS):
                sp.dma_start(adj_raw(t), adj_tile[t]).then_inc(adj_loaded[t], 16)
            for n, w in enumerate((Wq, Wk, Wv, Wo)):
                sp.dma_start(w_in[:, n, :], w).then_inc(w_loaded, 16)
            sp.dma_start(w1[:, :], W).then_inc(w_loaded, 16)
            for e in (0, 1):
                sp.dma_start(a_in[:, e:e + 1], a[e * D:(e + 1) * D, :]).then_inc(w_loaded, 16)
            for n, b in enumerate((bq, bk)):
                sp.dma_start(bias_col[:, n:n + 1], b.rearrange("(f o) -> f o", o=1)).then_inc(w_loaded, 16)
            for n, b in enumerate((bv, bo, gamma, beta)):
                row = b.rearrange("(o f) -> o f", o=1).broadcast_to([P, D])
                sp.dma_start(rows[:, n, :], row).then_inc(w_loaded, 16)
            for q in (0, 1):
                sp.dma_start(x_in[:, q], x_half[q]).then_inc(x_loaded, 16)

            def alone(semaphore, value):
                wait(sp, semaphore, value)
                if not isinstance(value, int):
                    stand_alone(sp)

            def stack(to, parts, picks, q, done):
                for h in range(HEADS):
                    for s, part in enumerate(picks):
                        sp.dma_start(to[s * DH:(s + 1) * DH, h, q * HALF:(q + 1) * HALF].bitcast(F32),
                                     parts[h * DH:(h + 1) * DH, part, :].bitcast(F32)).then_inc(done, 16)

            def half_of(tensor, b, q):
                row = b.times(2, q)
                if isinstance(row, int):
                    return tensor[row]
                return tensor[bass.ds(row, 1)].rearrange("o p t f -> (o p) t f")

            def iteration(i):
                for q in (0, 1):
                    f = i + -1
                    for c in range(CHUNKS):
                        if c == 0 and f.live():
                            if f.register is not None or f.offset > 0 or q:
                                before = count("turn_hidden1", i + -1) if q == 0 else count("turn_hidden0", i)
                                alone(work_done, before)
                                alone(x1_stored, f.times(32, 16 * q))
                            alone(h_stored, f.times(32, 16 * (q + 1)))
                            sp.dma_start(res[:, :, :], half_of(h_kept, f, q)).then_inc(res_loaded, 16)
                            sp.dma_start(h1[:, :, :], half_of(x_half, f, q)).then_inc(res_loaded, 16)
                        if (q, c) == (0, 2) and i.live():
                            alone(work_read, count("query1", i))
                            alone(scores_done, i.times(STEPS * HEADS))
                            stack(query_stack, query_parts, (0, 1, 0, 1), 1, queries_stacked)
                        if (q, c) == (1, 1) and (i + 1).live():
                            alone(work_read, count("query0", i))
                            alone(scores_done, slot((i, 0, 7), 3, 1))
                            stack(query_stack, query_parts, (0, 1, 0, 1), 0, queries_stacked)
                        if (q, c) == (1, 3) and (i + 1).live():
                            alone(work_read, count("key0", i))
                            alone(scores_done, slot((i, 1, 3), 3, 1))
                            stack(key_stack, key_parts, (0, 0, 1, 1), 0, keys_stacked)
                        if (q, c) == (1, 7) and (i + 1).live():
                            alone(work_read, count("key1", i))
                            alone(scores_done, slot((i, 1, 7), 3, 1))
                            stack(key_stack, key_parts, (0, 0, 1, 1), 1, keys_stacked)
                        if q == 0 and c in (4, 5) and (i + 1).live():
                            alone(normed[f"x{c - 4}"], (i + 1).times(1, 1))
                            sp.dma_start(half_of(h_kept, i + 1, c - 4), x_in[:, c - 4]).then_inc(h_stored, 16)
                        if (q, c) == (1, 5) and (i + 2).live():
                            alone(work_done, count("turn_x1", i))
                            alone(h_stored, (i + 2).times(32))
                            for half in (0, 1):
                                sp.dma_start(x_in[:, half], half_of(x_half, i + 2, half)).then_inc(x_loaded, 16)
                        if c == 6 and f.live():
                            alone(x1_ready, f.times(2, q + 1))
                            sp.dma_start(half_of(x1_kept, f, q), res[:, :, :]).then_inc(x1_stored, 16)
                        g, half = ((i + -3), 1) if q == 0 else ((i + -2), 0)
                        if c == (3 if q == 0 else 6) and g.live():
                            alone(work_done, count(f"gat_turn{half}", i))
                            alone(x1_stored, g.times(32, 16 * (half + 1)))
                            sp.dma_start(ring_tiles(TURN), half_of(x1_kept, g, half)).then_inc(x1_loaded, 16)
                        if c == (5 if q == 0 else 7) and g.live():
                            alone(out_ready, g.times(2, half + 1))
                            sp.dma_start(half_of(out_half, g, half), ring_tiles(OUT_A)).then_inc(out_stored, 16)

            iterations(sp, iteration)
            sp.wait_ge(h_stored, 32 * BATCHES)
            sp.wait_ge(x1_stored, 32 * BATCHES)
            sp.wait_ge(out_stored, 32 * BATCHES)

        @block.gpsimd
        def _(pool):
            nc.gpsimd.memset(eye[:, :], 0.0).then_inc(consts_step, 1)
            nc.gpsimd.memset(not_eye[:, :], 1.0).then_inc(consts_step, 1)
            nc.gpsimd.memset(one_of[:, :, :], 0.0).then_inc(consts_step, 1)
            nc.gpsimd.memset(pick[:, :], 0.0).then_inc(consts_step, 1)
            nc.gpsimd.memset(ones[:, :], 1.0).then_inc(consts_made, 1)
            nc.gpsimd.memset(eps[:, :], EPS).then_inc(consts_made, 1)
            nc.gpsimd.memset(minus_half[:, :], -0.5).then_inc(consts_made, 1)
            pool.wait_ge(consts_step, 4)
            nc.gpsimd.affine_select(out=eye[:, :], in_=eye[:, :], compare_op=ALU.not_equal, fill=1.0, base=0,
                                    pattern=[[-1, P]], channel_multiplier=1).then_inc(consts_step, 1)
            nc.gpsimd.affine_select(out=not_eye[:, :], in_=not_eye[:, :], compare_op=ALU.not_equal, fill=0.0,
                                    base=0, pattern=[[-1, P]], channel_multiplier=1).then_inc(consts_made, 1)
            picked = one_of[:, :, :].rearrange("p c d -> p (c d)")[:, 0:CHUNKS * DH:DH + 1]
            nc.gpsimd.memset(picked, 1.0).then_inc(consts_made, 1)
            for g in range(HEADS):
                pool.wait_ge(consts_made, 5 + g)
                nc.gpsimd.memset(pick[g * DH:g * DH + 1, :], 1.0).then_inc(consts_made, 1)
            pool.wait_ge(consts_step, 5)
            pool.wait_ge(consts_made, 9)
            nc.gpsimd.tensor_copy(eye_b[:, :], eye[:, :]).then_inc(consts_made, 1)
            pool.wait_ge(w_loaded, 16 * 13)
            pool.wait_ge(consts_made, 10)

            def rstd(s, n):
                _, moments, spread, scale, _ = norm[s]
                pool.wait_ge(moments_done[s], n)
                nc.gpsimd.tensor_tensor(spread[:, :], moments[:, :, 1], eps[:, :], ALU.add).then_inc(spread_done[s], 1)
                pool.wait_ge(spread_done[s], n)
                nc.gpsimd.tensor_tensor(scale[:, :], spread[:, :], minus_half[:, :], ALU.pow
                                        ).then_inc(rstd_done[s], 1)

            def hide(g, n):
                half, j = n // CHUNKS, n % CHUNKS
                pool.wait_ge(leaky_done, g.times(2 * CHUNKS, n + 1))
                nc.gpsimd.tensor_tensor(ring[:, n % RING, :], ring[:, n % RING, :],
                                        see_t[:, j, half * HALF:(half + 1) * HALF], ALU.add).then_inc(hidden_done, 1)

            def iteration(i):
                for q in (0, 1):
                    f = i + -1
                    for c in range(CHUNKS):
                        if c == 1 and f.live():
                            pool.wait_ge(res_loaded, f.times(64, 32 * (q + 1)))
                            nc.gpsimd.tensor_tensor(res[:, :, :], res[:, :, :],
                                                    rows[:, 1:2, :].broadcast_to([P, TILES, D]), ALU.add
                                                    ).then_inc(res_ready, 1)
                            nc.gpsimd.tensor_tensor(h1[:, :, :], h1[:, :, :],
                                                    rows[:, 3:4, :].broadcast_to([P, TILES, D]), ALU.add
                                                    ).then_inc(res_ready, 1)
                        if c == 4 and f.live():
                            pool.wait_ge(normed["y"], f.times(2, q + 1))
                            nc.gpsimd.tensor_tensor(res[:, :, :], res[:, :, :],
                                                    rows[:, 2:3, :].broadcast_to([P, TILES, D]), ALU.mult
                                                    ).then_inc(gamma_done, 1)
                            pool.wait_ge(gamma_done, f.times(2, q + 1))
                            pool.wait_ge(res_ready, f.times(4, 2 * q + 2))
                            nc.gpsimd.tensor_tensor(res[:, :, :], res[:, :, :], h1[:, :, :], ALU.add
                                                    ).then_inc(x1_ready, 1)
                        if q == 0 and c in (1, 2) and (i + 1).live():
                            rstd(f"x{c - 1}", (i + 1).times(1, 1))
                        if c == 3 and f.live():
                            rstd("y", f.times(2, q + 1))
                        if c == 5 and f.live():
                            rstd("z", f.times(2, q + 1))
                        g = i + -2
                        n = 0 if (q, c) == (0, 7) else 2 * c + 2 if q and c < 7 else None
                        if g.live() and n is not None:
                            hide(g, n)
                            hide(g, n + 1)

            iterations(pool, iteration)

        @block.scalar
        def _(act):
            act.wait_ge(w_turned, 1)
            nc.scalar.copy(w_t[:, :, :], ctx_ps[:, :].rearrange("p (t f) -> p t f", t=4)).then_inc(w_ready, 1)
            act.wait_ge(w_turned, 2)
            nc.scalar.copy(h1_t[:, 0:D], gat_ps[:, 0:D]).then_inc(w_ready, 1)
            act.wait_ge(w_turned, 3)
            nc.scalar.copy(w1_a[:, 0:2], sum_ps[:, 0:2]).then_inc(w_ready, 1)
            nc.scalar.mul(w1_a[:, 2:3], sum_ps[:, 1:2], 1 - SLOPE).then_inc(w_ready, 1)
            nc.scalar.mul(w1_a[:, 3:4], sum_ps[:, 1:2], SLOPE).then_inc(w_ready, 1)
            act.wait_ge(consts_made, 10)
            act.wait_ge(w_loaded, 16 * 13)

            def apply(s, n, to, source, function):
                _, _, _, scale, shift = norm[s]
                act.wait_ge(shift_done[s], n)
                for t in range(TILES):
                    last = nc.scalar.activation(to[:, t, :], source[:, t, :], function, bias=shift[:, t:t + 1],
                                                scale=scale[:, t:t + 1])
                last.then_inc(normed[s], 1)

            def leaky(g, n):
                half, j = n // CHUNKS, n % CHUNKS
                if n == RING:
                    act.wait_ge(work_done, count("gat_sums0", g + 2))
                if n == TURN:
                    wait(act, out_stored, g.times(32))
                nc.scalar.activation(ring[:, n % RING, :], from_row[:, half * HALF:(half + 1) * HALF], ACT.Relu,
                                     bias=ends[:, j, 2:3], scale=1 - SLOPE).then_inc(leaky_done, 1)

            def gat_exp(g, n):
                act.wait_ge(shifted_done, g.times(2 * CHUNKS, n + 1))
                nc.scalar.activation(ring[:, n % RING, :], ring[:, n % RING, :], ACT.Exp,
                                     bias=ends[:, n % CHUNKS, 3:4]).then_inc(gat_exp_done, 1)

            def read_gat(g, half):
                act.wait_ge(gat_done, g.times(2, half + 1))
                act.wait_ge(work_done, count(f"gat_sums{half}", g + 2 + half))
                wait(act, out_ready, g.times(2, half))
                nc.scalar.copy(ring[:, TURN, :], gat_ps[:, :]).then_inc(gat_read, 1)

            def at(i, q, c, j):
                step = next_step(i, q, c)
                if step[0].live():
                    act.wait_ge(scores_done, slot(step, j, 1))
                    nc.scalar.activation(score[:, j, :], score[:, j, :], ACT.Exp, scale=DH ** -0.5
                                         ).then_inc(exp_done, 1)
                done = last_step(i, q, c)
                if j == 1 and c == 0 and done[0].live():
                    act.wait_ge(sums_done, number(done, 1))
                    nc.scalar.copy(sums[:, :], sum_ps[:, :]).then_inc(sums_read, 1)
                name, off = JOB_AT.get((q, c, j), (None, 0))
                if name and (i + off).live():
                    if name.startswith("gather") or name.startswith("turn_sums") or name == "ends" or \
                            name.startswith("project") or name.startswith("value") or \
                            name.startswith("gat_turn"):
                        pass
                    elif name.startswith("query") or name.startswith("key"):
                        is_key = name.startswith("key")
                        parts = key_parts if is_key else query_parts
                        b = i + off
                        half = int(name[-1])
                        act.wait_ge(work_done, count(name, i))
                        wait(act, keys_stacked if is_key else queries_stacked, b.times(512, 256 * half))
                        nc.scalar.activation(parts[:, 0, :], work[:, :], ACT.Identity,
                                             bias=bias_col[:, int(is_key):int(is_key) + 1]).then_inc(high_ready, 1)
                    else:
                        act.wait_ge(work_done, count(name, i))
                        if name.startswith("turn_context"):
                            to = context_t[:, :]
                        elif name.startswith("turn_hidden"):
                            to = h1_t[:, q * HALF:(q + 1) * HALF]
                        elif name.startswith("turn_x"):
                            half = int(name[-1])
                            to = h_t[:, half * HALF:(half + 1) * HALF]
                        elif name.startswith("wh"):
                            half = int(name[-1])
                            to = wh[:, half * TILES:(half + 1) * TILES, :].rearrange("p t f -> p (t f)")
                        elif name.startswith("to_row"):
                            half = int(name[-1])
                            wait(act, shifted_done, (i + off).times(2 * CHUNKS))
                            to = to_row[:, half * HALF:(half + 1) * HALF]
                        elif name.startswith("peak_row"):
                            half = int(name[-1])
                            to = to_row[:, half * HALF:(half + 1) * HALF]
                        elif name.startswith("from_row"):
                            half = int(name[-1])
                            to = from_row[:, half * HALF:(half + 1) * HALF]
                        else:
                            assert name.startswith("gat_sums"), name
                            to = ring[:, SUMS, :]
                        nc.scalar.copy(to, work[:, :]).then_inc(work_read, 1)
                if j == 3 and done[0].live():
                    act.wait_ge(context_done, number(done, 1))
                    earlier = done[0] + -1 if done[1] == 0 else done[0]
                    if earlier.live():
                        act.wait_ge(work_done, count(f"gather_last{q}" if c == 0 else f"gather{q}{c - 1}", i))
                    nc.scalar.copy(context[:, done[2], :], ctx_ps[:, :]).then_inc(context_read, 1)
                f = i + -1
                if f.live():
                    n = f.times(2, q + 1)
                    if (c, j) == (4, 0):
                        apply("y", n, res, res, ACT.Identity)
                    if (c, j) == (6, 0):
                        apply("z", n, h1, res, ACT.Relu)
                if q == 0 and (i + 1).live():
                    for half, at_apply in enumerate(((2, 2), (3, 3))):
                        n = (i + 1).times(1, 1)
                        if (c, j) == at_apply:
                            apply(f"x{half}", n, x_in[:, half], x_in[:, half], ACT.Relu)
                g = i + -2
                if g.live():
                    if j in (0, 2) and ((q, c) == (0, 7) or q and c < 7):
                        leaky(g, j // 2 + (0 if q == 0 else 2 * c + 2))
                    if q and j == 3:
                        gat_exp(g, 2 * c)
                    if q and c and j == 1:
                        gat_exp(g, 2 * c - 1)
                    if (q, c, j) == (1, 6, 2):
                        act.wait_ge(negative_ready, g.times(2, 1))
                        nc.scalar.activation(ring[:, OUT_B, :], ring[:, OUT_B, :], ACT.Exp).then_inc(negative_exp, 1)
                    if (q, c, j) == (1, 5, 0):
                        read_gat(g, 0)
                g = i + -3
                if g.live():
                    if (q, c, j) == (0, 0, 1):
                        gat_exp(g, 2 * CHUNKS - 1)
                    if (q, c, j) == (0, 1, 2):
                        read_gat(g, 1)
                    if (q, c, j) == (0, 4, 0):
                        act.wait_ge(negative_ready, g.times(2, 2))
                        nc.scalar.activation(ring[:, OUT_B, :], ring[:, OUT_B, :], ACT.Exp).then_inc(negative_exp, 1)

            def iteration(i):
                for q in (0, 1):
                    for c in range(CHUNKS):
                        for j in range(HEADS):
                            at(i, q, c, j)

            iterations(act, iteration)

        @block.vector
        def _(dve):
            dve.wait_ge(consts_made, 10)
            for t in range(CHUNKS):
                dve.wait_ge(adj_loaded[t], 16)
                if t >= 2:
                    dve.wait_ge(adj_turned, t - 1)
                nc.vector.tensor_copy(adj_bf16(t), adj_raw(t)).then_inc(adj_cast, 1)
                nc.vector.tensor_scalar(see[:, t, :], adj_raw(t), 0.0, OUT_OF_SIGHT, ALU.is_le, ALU.mult
                                        ).then_inc(masks_step, 1)
                dve.wait_ge(adj_turned, t + 1)
                nc.vector.tensor_scalar(cap[:, :, t * P:(t + 1) * P], adj_turned_ps(t), 0.0, HIGH,
                                        ALU.not_equal, ALU.mult).then_inc(masks_step, 1)
                nc.vector.tensor_scalar(see_t[:, :, t * P:(t + 1) * P], adj_turned_ps(t), 0.0, OUT_OF_SIGHT,
                                        ALU.is_le, ALU.mult).then_inc(adj_used, 1)
            dve.wait_ge(masks_step, 2 * CHUNKS)
            dve.wait_ge(adj_used, CHUNKS)
            for t in range(CHUNKS):
                for m in (see, see_t):
                    spot = m[:, t, t * P:(t + 1) * P]
                    nc.vector.tensor_tensor(spot, spot, not_eye[:, :], ALU.mult).then_inc(masks_step, 1)
                nc.vector.tensor_scalar(cap[:, t, :], cap[:, t, :], LOW, None, ALU.max).then_inc(masks_step, 1)
            dve.wait_ge(masks_step, 5 * CHUNKS)
            dve.wait_ge(w_loaded, 16 * 13)

            def moments(s, n, source):
                stats, moment, _, _, _ = norm[s]
                for t in range(TILES):
                    last = nc.vector.bn_stats(stats[:, t, :], source[:, t, :])
                last.then_inc(stats_done[s], 1)
                dve.wait_ge(stats_done[s], n)
                stand_alone(dve)
                for t in range(TILES):
                    last = nc.vector.bn_aggr(moment[:, t, :], stats[:, t, :])
                last.then_inc(moments_done[s], 1)

            def shift(s, n):
                _, moment, _, scale, to = norm[s]
                dve.wait_ge(rstd_done[s], n)
                nc.vector.scalar_tensor_tensor(out=to[:, :], in0=moment[:, :, 0], scalar=-1.0, in1=scale[:, :],
                                               op0=ALU.mult, op1=ALU.mult).then_inc(shift_done[s], 1)

            def heads(tile):
                return tile.rearrange("p t (h d) -> p t h d", h=HEADS)

            def gather(i, name, b, q, chunk):
                to = gathered if chunk == 0 else scaled
                wait(dve, gathered_step, b.times(14, 7 * q + max(chunk - 1, 0)))
                dve.wait_ge(work_done, count(name, i))
                share = inverse[:, :, :, chunk:chunk + 1].broadcast_to([P, TILES, HEADS, DH])
                nc.vector.tensor_tensor(heads(to[:, :, :]), heads(work_tiles), share, ALU.mult
                                        ).then_inc(work_read, 1)
                if chunk:
                    dve.wait_ge(work_read, count(name, i))
                    nc.vector.tensor_tensor(gathered[:, :, :], gathered[:, :, :], scaled[:, :, :], ALU.add
                                            ).then_inc(gathered_step, 1)

            def see_peak(g, t):
                if t:
                    dve.wait_ge(peak_step, g.times(PEAK_STEPS, t))
                    stand_alone(dve)
                nc.vector.tensor_tensor_reduce(
                    out=ring[:, RING - 2:RING, :].rearrange("p a n -> p (a n)"), in0=to_row[:, :], in1=see[:, t, :],
                    scale=1.0, scalar=-3e38, op0=ALU.add, op1=ALU.max, accum_out=peak[:, t:t + 1]
                ).then_inc(peak_step, 1)

            def divide_gat(i, g, half):
                dve.wait_ge(work_done, count(f"gat_turn{half}", i))
                wait(dve, out_stored, g.times(32, 16 * half))
                nc.vector.tensor_tensor(ring_tiles(OUT_A), work_tiles,
                                        gat_inverse[:, :].unsqueeze(2).broadcast_to([P, TILES, D]), ALU.mult
                                        ).then_inc(work_read, 1)
                dve.wait_ge(work_read, count(f"gat_turn{half}", i))
                nc.vector.tensor_scalar(ring[:, OUT_B, :], ring[:, OUT_A, :], 0.0, None, ALU.min
                                        ).then_inc(negative_ready, 1)

            def elu(g, half):
                dve.wait_ge(negative_exp, g.times(2, half + 1))
                nc.vector.scalar_tensor_tensor(out=ring[:, OUT_B, :], in0=ring[:, OUT_A, :], scalar=0.0,
                                               in1=ring[:, OUT_B, :], op0=ALU.max, op1=ALU.add).then_inc(elu_step, 1)
                dve.wait_ge(x1_loaded, g.times(32, 16 * (half + 1)))
                dve.wait_ge(elu_step, g.times(2, half + 1))
                nc.vector.scalar_tensor_tensor(out=ring[:, OUT_A, :], in0=ring[:, OUT_B, :], scalar=-1.0,
                                               in1=ring[:, TURN, :], op0=ALU.add, op1=ALU.add).then_inc(out_ready, 1)

            def at(i, q, c, j):
                step = next_step(i, q, c)
                if step[0].live():
                    if j == 0:
                        wait(dve, sums_done, number(step, -1))
                    dve.wait_ge(exp_done, slot(step, j, 1))
                    nc.vector.scalar_tensor_tensor(
                        out=probs[:, step[2] % 2, j, :], in0=score[:, j, :], scalar=LOW,
                        in1=cap[:, step[2], step[1] * HALF:(step[1] + 1) * HALF],
                        op0=ALU.max, op1=ALU.min).then_inc(probs_ready, 1)
                name, off = JOB_AT.get((q, c, j), (None, 0))
                if name and (i + off).live():
                    if name.startswith("gather_last"):
                        gather(i, name, i + off, q, CHUNKS - 1)
                    elif name.startswith("gather"):
                        gather(i, name, i + off, 1 - q, c - 1)
                    elif name.startswith("turn_sums"):
                        dve.wait_ge(work_done, count(name, i))
                        found = work[:, :].rearrange("p (t h r) -> p t h r", t=TILES, h=HEADS)[:, :, :, 0:CHUNKS]
                        nc.vector.reciprocal(inverse[:, :, :, :], found).then_inc(work_read, 1)
                    elif name.startswith("query") or name.startswith("key"):
                        is_key = name.startswith("key")
                        parts = key_parts if is_key else query_parts
                        b, half = i + off, int(name[-1])
                        turn = {"query0": 1, "key0": 2, "key1": 3, "query1": 4}[name]
                        dve.wait_ge(high_ready, b.times(4, turn))
                        nc.vector.scalar_tensor_tensor(
                            out=parts[:, 1, :], in0=work[:, :], scalar=bias_col[:, int(is_key):int(is_key) + 1],
                            in1=parts[:, 0, :].bitcast(F32), op0=ALU.add, op1=ALU.subtract).then_inc(work_read, 1)
                    elif name.startswith("value"):
                        half = int(name[-1])
                        dve.wait_ge(work_done, count(name, i))
                        nc.vector.tensor_tensor(value[:, half * TILES:(half + 1) * TILES, :], work_tiles,
                                                rows[:, 0:1, :].broadcast_to([P, TILES, D]), ALU.add
                                                ).then_inc(work_read, 1)
                    elif name.startswith("project"):
                        f = i + off
                        dve.wait_ge(work_done, count(name, i))
                        dve.wait_ge(res_ready, f.times(4, 2 * q + 1))
                        nc.vector.tensor_tensor(res[:, :, :], work_tiles, res[:, :, :], ALU.add).then_inc(work_read, 1)
                        dve.wait_ge(work_read, count(name, i))
                        moments("y", f.times(2, q + 1), res)
                    elif name == "ends":
                        dve.wait_ge(work_done, count(name, i))
                        nc.vector.tensor_copy(ends[:, :, :].rearrange("p t e -> p (t e)"), work[:, 0:4 * CHUNKS]
                                              ).then_inc(work_read, 1)
                    elif name.startswith("gat_turn_sums"):
                        dve.wait_ge(work_done, count(name, i))
                        nc.vector.reciprocal(gat_inverse[:, :], work[:, 0:TILES]).then_inc(work_read, 1)
                    elif name.startswith("gat_turn"):
                        divide_gat(i, i + off, int(name[-1]))
                f = i + -1
                if f.live():
                    n = f.times(2, q + 1)
                    if (c, j) == (3, 2):
                        shift("y", n)
                    if (c, j) == (5, 0):
                        dve.wait_ge(x1_ready, n)
                        moments("z", n, res)
                    if (c, j) == (5, 3):
                        shift("z", n)
                if q == 0 and (i + 1).live():
                    for half, (c0, j0, c1, j1) in enumerate(((1, 0, 2, 0), (2, 2, 3, 1))):
                        n = (i + 1).times(1, 1)
                        if (c, j) == (c0, j0):
                            dve.wait_ge(x_loaded, (i + 1).times(32, 32))
                            moments(f"x{half}", n, x_in[:, half])
                        if (c, j) == (c1, j1):
                            shift(f"x{half}", n)
                g = i + -2
                if g.live():
                    if q == 0 and 4 <= c <= 6:
                        if (c, j) == (4, 0):
                            dve.wait_ge(work_read, count("ends", i))
                            stand_alone(dve)
                        first = {4: 0, 5: 3, 6: 6}[c]
                        if j < 3 and first + j < CHUNKS:
                            see_peak(g, first + j)
                        if (c, j) == (6, 2):
                            dve.wait_ge(peak_step, g.times(PEAK_STEPS, CHUNKS))
                            nc.vector.tensor_tensor(peak[:, :], peak[:, :], ends[:, :, 0], ALU.add
                                                    ).then_inc(peak_step, 1)
                            dve.wait_ge(peak_step, g.times(PEAK_STEPS, CHUNKS + 1))
                            nc.vector.tensor_scalar(peak[:, :], peak[:, :], -1.0, None, ALU.mult
                                                    ).then_inc(peak_step, 1)
                            dve.wait_ge(peak_step, g.times(PEAK_STEPS, CHUNKS + 2))
                            nc.vector.scalar_tensor_tensor(out=peak[:, :], in0=peak[:, :], scalar=SLOPE,
                                                           in1=peak[:, :], op0=ALU.mult, op1=ALU.min
                                                           ).then_inc(peak_step, 1)
                            dve.wait_ge(peak_step, g.times(PEAK_STEPS, CHUNKS + 3))
                            nc.vector.scalar_tensor_tensor(out=row_shift[:, :], in0=ends[:, :, 0], scalar=SLOPE,
                                                           in1=peak[:, :], op0=ALU.mult, op1=ALU.add
                                                           ).then_inc(peak_done, 1)
                    if q and j in (1, 3):
                        n = 2 * c + j // 2
                        half = n // CHUNKS
                        dve.wait_ge(hidden_done, g.times(2 * CHUNKS, n + 1))
                        if n == 0:
                            dve.wait_ge(work_read, count("peak_row1", i))
                        nc.vector.tensor_tensor(ring[:, n % RING, :], ring[:, n % RING, :],
                                                to_row[:, half * HALF:(half + 1) * HALF], ALU.add
                                                ).then_inc(shifted_done, 1)
                    if (q, c, j) == (1, 7, 0):
                        elu(g, 0)
                g = i + -3
                if g.live() and (q, c, j) == (0, 4, 2):
                    elu(g, 1)

            def iteration(i):
                for q in (0, 1):
                    for c in range(CHUNKS):
                        for j in range(HEADS):
                            at(i, q, c, j)

            iterations(dve, iteration)

        @block.tensor
        def _(pe):
            pe.wait_ge(w_loaded, 16 * 13)
            pe.wait_ge(consts_made, 10)
            for n in range(4):
                last = nc.tensor.transpose(ctx_ps[:, n * D:(n + 1) * D], w_in[:, n, :], eye[:, :])
            last.then_inc(w_turned, 1)
            nc.tensor.transpose(gat_ps[:, 0:D], w1[:, :], eye[:, :]).then_inc(w_turned, 1)
            pe.wait_ge(w_ready, 2)
            nc.tensor.matmul(sum_ps[:, 0:2], h1_t[:, 0:D], a_in[:, :], start=True, stop=True).then_inc(w_turned, 1)
            for t in range(CHUNKS):
                pe.wait_ge(adj_cast, t + 1)
                if t >= 4:
                    pe.wait_ge(adj_used, t - 3)
                for jt in range(CHUNKS):
                    last = nc.tensor.transpose(adj_turned_ps(t)[:, jt, :], adj_bf16(t)[:, jt * P:(jt + 1) * P],
                                               eye_b[:, :])
                last.then_inc(adj_turned, 1)
            pe.wait_ge(w_ready, 5)
            pe.wait_ge(adj_used, CHUNKS)

            def turn(source):
                for t in range(TILES):
                    last = nc.tensor.transpose(work[:, t * P:(t + 1) * P], source(t), eye[:, :])
                return last

            def product(pairs):
                for t, (left, right) in enumerate(pairs):
                    last = nc.tensor.matmul(work[:, t * P:(t + 1) * P], left, right, start=True, stop=True)
                return last

            def job(i, name, b, q, c):
                wait(pe, work_read, count(name, i) + -1)
                half = int(name[-1]) if name[-1].isdigit() else 0
                side = slice(half * HALF, (half + 1) * HALF)
                if name.startswith("gather"):
                    chunk = CHUNKS - 1 if c == 0 else c - 1
                    pe.wait_ge(context_read, number((b, q if c == 0 else 1 - q, chunk), 1))
                    last = turn(lambda t: context[:, chunk, t * P:(t + 1) * P])
                elif name.startswith("turn_sums"):
                    pe.wait_ge(sums_read, b.times(2, (1 - q) + 1))
                    last = turn(lambda t: sums[:, t * P:(t + 1) * P])
                elif name.startswith("turn_context"):
                    pe.wait_ge(gathered_step, b.times(14, 7 * (q + 1)))
                    last = turn(lambda t: gathered[:, t, :])
                elif name.startswith("project"):
                    last = product([(context_t[:, t * P:(t + 1) * P], w_t[:, 3, :]) for t in range(TILES)])
                elif name.startswith("turn_hidden"):
                    pe.wait_ge(normed["z"], b.times(2, q + 1))
                    last = turn(lambda t: h1[:, t, :])
                elif name.startswith("turn_x"):
                    pe.wait_ge(normed[f"x{half}"], b.times(1, 1))
                    last = turn(lambda t: x_in[:, half, t, :])
                elif name.startswith("query"):
                    last = nc.tensor.matmul(work[:, :], w_t[:, 0, :], h_t[:, side], start=True, stop=True)
                elif name.startswith("key"):
                    last = nc.tensor.matmul(work[:, :], w_t[:, 1, :], h_t[:, side], start=True, stop=True)
                elif name.startswith("value"):
                    last = product([(h_t[:, (half * TILES + t) * P:(half * TILES + t + 1) * P], w_t[:, 2, :])
                                    for t in range(TILES)])
                elif name.startswith("wh"):
                    last = product([(h1_t[:, (half * TILES + t) * P:(half * TILES + t + 1) * P], w1[:, :])
                                    for t in range(TILES)])
                elif name == "ends":
                    for t in range(CHUNKS):
                        last = nc.tensor.matmul(work[:, 4 * t:4 * t + 4], h1_t[:, t * P:(t + 1) * P], w1_a[:, :],
                                                start=True, stop=True)
                elif name.startswith("to_row"):
                    last = nc.tensor.matmul(work[:, :], w1_a[:, 1:2].broadcast_to([P, P]), h1_t[:, side],
                                            start=True, stop=True)
                elif name.startswith("from_row"):
                    last = nc.tensor.matmul(work[:, :], w1_a[:, 0:1].broadcast_to([P, P]), h1_t[:, side],
                                            start=True, stop=True)
                elif name.startswith("peak_row"):
                    pe.wait_ge(peak_done, b.times(1, 1))
                    last = product([(row_shift[:, half * TILES + t:half * TILES + t + 1].broadcast_to([P, P]),
                                     eye[:, :]) for t in range(TILES)])
                elif name.startswith("gat_sums"):
                    for jt in range(CHUNKS):
                        g = jt % 4
                        last = nc.tensor.matmul(work[g * DH:(g + 1) * DH, :], ones[:, :],
                                                ring[:, (half * CHUNKS + jt) % RING, :],
                                                start=jt < 4, stop=jt >= 4)
                elif name.startswith("gat_turn_sums"):
                    for t in range(TILES):
                        last = nc.tensor.matmul(work[:, t:t + 1], ring[:, SUMS, t * P:(t + 1) * P], pick[:, :],
                                                start=True, stop=True)
                else:
                    assert name.startswith("gat_turn"), name
                    pe.wait_ge(gat_read, b.times(2, half + 1))
                    last = turn(lambda t: ring[:, TURN, t * P:(t + 1) * P])
                last.then_inc(work_done, 1)

            def neighbours(g, n):
                half, jt = n // CHUNKS, n % CHUNKS
                pe.wait_ge(gat_exp_done, g.times(2 * CHUNKS, n + 1))
                if jt == 0:
                    wait(pe, gat_read, g.times(2, half))
                last = nc.tensor.matmul(gat_ps[:, :], wh[:, jt, :], ring[:, n % RING, :], start=jt == 0,
                                        stop=jt == CHUNKS - 1)
                if jt == CHUNKS - 1:
                    last.then_inc(gat_done, 1)

            def at(i, q, c, j):
                step, done = next_step(i, q, c), last_step(i, q, c)
                if step[0].live():
                    b, sq, sc = step
                    if j == 0 and sc == 0:
                        pe.wait_ge(queries_stacked, b.times(512, 256 * (sq + 1)))
                    if j == 0 and sq == 0 and sc in (0, TILES):
                        pe.wait_ge(keys_stacked, b.times(512, 256 * (sc // TILES + 1)))
                    wait(pe, probs_ready, slot(step, j, 1 - HEADS))
                    nc.tensor.matmul(score[:, j, :], key_stack[:, j, sc * P:(sc + 1) * P],
                                     query_stack[:, j, sq * HALF:(sq + 1) * HALF], start=True, stop=True
                                     ).then_inc(scores_done, 1)
                if done[0].live() and j == 0:
                    pe.wait_ge(probs_ready, slot(done, HEADS))
                    wait(pe, context_read, number(done))
                    for h in range(HEADS):
                        last = nc.tensor.matmul(ctx_ps[h * DH:(h + 1) * DH, :],
                                                value[:, done[2], h * DH:(h + 1) * DH],
                                                probs[:, done[2] % 2, h, :], start=True, stop=True)
                    last.then_inc(context_done, 1)
                if done[0].live() and j == 1:
                    if done[2] == 0:
                        wait(pe, sums_read, done[0].times(2, done[1]))
                    for h in range(HEADS):
                        last = nc.tensor.matmul(sum_ps[h * DH:(h + 1) * DH, :], one_of[:, done[2], :],
                                                probs[:, done[2] % 2, h, :], start=done[2] == 0,
                                                stop=done[2] == CHUNKS - 1)
                    last.then_inc(sums_done, 1)
                name, off = JOB_AT.get((q, c, j), (None, 0))
                if name and (i + off).live():
                    job(i, name, i + off, q, c)
                if j in (0, 2):
                    if q and c and (i + -2).live():
                        neighbours(i + -2, 2 * c - 2 + j // 2)
                    if (q, c) == (0, 0) and (i + -3).live():
                        neighbours(i + -3, 2 * CHUNKS - 2 + j // 2)

            def iteration(i):
                for q in (0, 1):
                    for c in range(CHUNKS):
                        for j in range(HEADS):
                            at(i, q, c, j)

            iterations(pe, iteration)


_INS = ["x", "adj", "L0_gnn_Wq", "L0_gnn_bq", "L0_gnn_Wk", "L0_gnn_bk", "L0_gnn_Wv", "L0_gnn_bv", "L0_gnn_Wo",
        "L0_gnn_bo", "L0_gnn_gamma", "L0_gnn_beta", "L1_gnn_W", "L1_gnn_a"]


def kernel(**inputs):
    import numpy as np
    import concourse.bacc as bacc
    from concourse.bass_utils import run_bass_kernel_spmd

    nc = bacc.Bacc("TRN2", target_bir_lowering=False, num_devices=1)
    arrays, args = {}, []
    for name in _INS:
        array = np.ascontiguousarray(inputs[name])
        arrays[f"in_{name}"] = array
        args.append(nc.dram_tensor(f"in_{name}", array.shape, mybir.dt.from_np(array.dtype), kind="ExternalInput").ap())
    args.append(nc.dram_tensor("out_0", (BATCHES, N, D), F32, kind="ExternalOutput").ap())
    build(nc, *args)
    result = run_bass_kernel_spmd(nc, [arrays], core_ids=[0])
    return result.results[0]["out_0"]
```

```python
from contextlib import ExitStack

import concourse.bass as bass
from concourse import mybir

F32 = mybir.dt.float32
F32R = mybir.dt.float32r
BF16 = mybir.dt.bfloat16
I32 = mybir.dt.int32
ALU = mybir.AluOpType
ACT = mybir.ActivationFunctionType

P = 128
BATCHES, N, D = 8, 1024, 128
HEADS = 4
DH = D // HEADS
CHUNKS = N // P
HALF = N // 2
TILES = HALF // P
STEPS = 2 * CHUNKS
EPS = 1e-5
LOW, HIGH = 4.5399929762484854e-05, 22026.465794806718
OUT_OF_SIGHT = -1e30
SLOPE = 0.2
RING = 12
SCORES = 3
PEAKS_AT = [(3, 1), (3, 3), (4, 0), (4, 1), (4, 3), (5, 0), (5, 1), (5, 3)]
PEAK_STEPS = CHUNKS + 3
MASKS_AT = [(0, 5, 3), (0, 6, 3), (0, 7, 3), (1, 0, 3), (1, 2, 0), (1, 3, 0), (1, 4, 0), (1, 5, 0), (1, 6, 0)]
TURN, SUMS, OUT_A, OUT_B = 4, 5, 6, 7

JOBS = sorted(
    [(q, 0, 0, f"turn_sums{q}", q - 1) for q in (0, 1)]
    + [(q, 0, 1, f"turn_context{q}", -1) for q in (0, 1)]
    + [(q, c, 0 if c else 2, f"gather{q}{c}", q - 1) for q in (0, 1) for c in range(CHUNKS)]
    + [(q, 2, 1, f"project{q}", -1) for q in (0, 1)]
    + [(q, 7, 3, f"turn_hidden{q}", -1) for q in (0, 1)]
    + [
        (0, 0, 3, "to_row0", -2), (0, 1, 1, "gat_sums1", -3), (0, 1, 2, "to_row1", -2), (0, 1, 3, "value1", 0),
        (0, 2, 2, "gat_turn_sums1", -3), (0, 2, 3, "ends", -2), (0, 3, 1, "query1", 0),
        (0, 3, 2, "gat_turn1", -3), (0, 3, 3, "wh0", -2), (0, 4, 1, "wh1", -2),
        (0, 4, 2, "turn_x0", 1), (0, 5, 2, "turn_x1", 1),
        (0, 6, 1, "near_row0", -2), (0, 6, 3, "base_row0", -2), (0, 7, 1, "near_row1", -2),
        (0, 7, 2, "base_row1", -2),
        (1, 1, 1, "query0", 1), (1, 1, 3, "key0", 1), (1, 4, 1, "key1", 1), (1, 4, 3, "gat_sums0", -2),
        (1, 5, 2, "gat_turn_sums0", -2), (1, 5, 3, "value0", 1), (1, 6, 1, "gat_turn0", -2),
    ]
)
JOB_AT = {(q, c, j): (name, off) for q, c, j, name, off in JOBS}
ORDER = {name: n for n, (_, _, _, name, _) in enumerate(JOBS)}
OFFSET = {name: off for _, _, _, name, off in JOBS}
FIRST, LAST = -1, BATCHES + 2
LOOP = range(3, BATCHES - 2)
READ_BY_VECTOR = ("gather", "turn_sums", "ends", "project", "value", "gat_turn")


class Graph:

    def __init__(self, offset, register=None):
        self.offset, self.register = offset, register

    def __add__(self, n):
        return Graph(self.offset + n, self.register)

    def live(self):
        return self.register is not None or 0 <= self.offset < BATCHES

    def times(self, k, plus=0):
        constant = self.offset * k + plus
        return constant if self.register is None else self.register * k + constant


def jobs_of(i, bank):
    return [n for n, (_, _, _, _, off) in enumerate(JOBS) if n % 2 == bank and 0 <= i + off < BATCHES]


def jobs_before(i, bank):
    return sum(len(jobs_of(k, bank)) for k in range(FIRST, i))


def bank_of(name):
    return ORDER[name] % 2


def count(name, i):
    n, bank = ORDER[name], bank_of(name)
    if i.register is None:
        return jobs_before(i.offset, bank) + sum(m <= n for m in jobs_of(i.offset, bank))
    everyone = range(bank, len(JOBS), 2)
    if i.offset < 0:
        missing = set(everyone) - set(jobs_of(LOOP[0] - 1, bank))
        assert i.offset == -1 and all(m < n for m in missing), name
    at = Graph(i.offset - LOOP[0], i.register)
    return at.times(len(everyone), jobs_before(LOOP[0], bank) + n // 2 + 1)


def iterations(engine, body):
    for i in range(FIRST, LOOP[0]):
        body(Graph(i))
    with engine.Fori(LOOP[0], LOOP[-1] + 1) as register:
        body(Graph(0, register))
    for i in range(LOOP[-1] + 1, LAST + 1):
        body(Graph(i))


def moved(i, q, c, j, places):
    n = (q * CHUNKS + c) * HEADS + j + places
    whole, n = divmod(n, STEPS * HEADS)
    return (i + whole if whole else i), n // (CHUNKS * HEADS), n // HEADS % CHUNKS, n % HEADS


def ahead(i, q, c, j, places):
    i, q, c, h = moved(i, q, c, j, places)
    return (i, q, c), h


def score_bank(step, h):
    n = (step[1] * CHUNKS + step[2]) * HEADS + h
    last = STEPS * HEADS - 1
    bank = 1 if n == last else n % SCORES
    back = {0: 4, 1: 2, 2: 4, last: 2}.get(n, SCORES)
    return bank, back


def slot(step, h, plus=0):
    i, q, c = step
    return i.times(STEPS * HEADS, (q * CHUNKS + c) * HEADS + h + plus)


def number(step, plus=0):
    i, q, c = step
    return i.times(STEPS, q * CHUNKS + c + plus)


def build(nc, x, adj, Wq, bq, Wk, bk, Wv, bv, Wo, bo, gamma, beta, W, a, out):
    x_half = x.rearrange("b (h t p) f -> (b h) p t f", h=2, p=P)
    out_half = out.rearrange("b (h t p) f -> (b h) p t f", h=2, p=P)
    adj_tile = adj.rearrange("(t p) j -> t p j", p=P)
    h_kept = nc.dram_tensor("h_kept", (2 * BATCHES, P, TILES, D), F32, kind="Internal").ap()
    x1_kept = nc.dram_tensor("x1_kept", (2 * BATCHES, P, TILES, D), F32, kind="Internal").ap()

    ctx = ExitStack()
    with ctx:

        def sb(name, shape, dt=F32):
            return ctx.enter_context(nc.sbuf_tensor(name, shape, dt))

        def pb(name, shape, dt=F32):
            return ctx.enter_context(nc.psum_tensor(name, shape, dt))

        def sem(name):
            return ctx.enter_context(nc.semaphore(name))

        cap = sb("cap", [P, CHUNKS, N])
        see_t = sb("see_t", [P, CHUNKS, N], BF16)
        see = sb("see", [P, CHUNKS, N], BF16)
        key_stack = sb("key_stack", [P, HEADS, N], F32R)
        query_stack = sb("query_stack", [P, HEADS, N], F32R)
        key_parts = sb("key_parts", [P, 2, HALF], F32R)
        query_parts = sb("query_parts", [P, 2, HALF], F32R)
        value = sb("value", [P, CHUNKS, D])
        probs = sb("probs", [P, 2, HEADS, HALF])
        context = sb("context", [P, CHUNKS, HALF])
        sums = sb("sums", [P, HALF])
        inverse = sb("inverse", [P, TILES, HEADS, CHUNKS])
        gathered = sb("gathered", [P, TILES, D])
        scaled = sb("scaled", [P, TILES, D])
        context_t = sb("context_t", [P, HALF])
        x_in = sb("x_in", [P, 2, TILES, D])
        h_t = sb("h_t", [P, N])
        res = sb("res", [P, TILES, D])
        h1 = sb("h1", [P, TILES, D])
        h1_t = sb("h1_t", [P, N])
        wh = sb("wh", [P, CHUNKS, D])
        near_row = sb("near_row", [P, N])
        to_row = sb("to_row", [P, N])
        ends = sb("ends", [P, CHUNKS, 4])
        peak = sb("peak", [P, CHUNKS])
        row_shift = sb("row_shift", [P, 2, CHUNKS])
        gat_inverse = sb("gat_inverse", [P, TILES])
        ring = sb("ring", [P, RING, HALF])
        w_in = h_t[:, 0:4 * D].rearrange("p (n f) -> p n f", n=4)
        w_t = sb("w_t", [P, 4, D])
        w1 = sb("w1", [P, D])
        a_in = sb("a_in", [P, 2])
        w1_a = sb("w1_a", [P, 4])
        bias_col = sb("bias_col", [P, 2])
        rows = sb("rows", [P, 4, D])
        eye = sb("eye", [P, P])
        eye_b = ring[:, 3, 0:P // 2].bitcast(BF16)
        not_eye = ring[:, 2, 0:P // 2].bitcast(BF16)
        one_of = sb("one_of", [P, CHUNKS, DH])
        ones = sb("ones", [P, DH])
        pick = sb("pick", [P, 1])
        eps = sb("eps", [P, TILES])
        minus_half = sb("minus_half", [P, TILES])
        small = sb("small", [P, 4, TILES * 11])
        norm = {}
        for n, s in enumerate(("x0", "x1", "y", "z")):
            norm[s] = (small[:, n, 0:24].rearrange("p (t k) -> p t k", t=TILES),
                       small[:, n, 24:32].rearrange("p (t k) -> p t k", t=TILES),
                       small[:, n, 32:36], small[:, n, 36:40], small[:, n, 40:44])

        score = pb("score", [P, SCORES, HALF])
        ctx_ps = pb("ctx_ps", [P, HALF])
        sum_ps = pb("sum_ps", [P, HALF])
        work = pb("work", [P, 2, HALF])
        gat_ps = pb("gat_ps", [P, HALF])

        def in_tiles(bank):
            return work[:, bank, :].rearrange("p (t f) -> p t f", t=TILES)

        w_loaded = sem("w_loaded")
        adj_loaded = [sem(f"adj_loaded{t}") for t in range(CHUNKS)]
        x_loaded = sem("x_loaded")
        h_stored = sem("h_stored")
        res_loaded = sem("res_loaded")
        x1_stored = sem("x1_stored")
        x1_loaded = sem("x1_loaded")
        out_stored = sem("out_stored")
        keys_stacked = sem("keys_stacked")
        queries_stacked = sem("queries_stacked")
        consts_made = sem("consts_made")
        consts_step = sem("consts_step")
        adj_cast = sem("adj_cast")
        see_made = sem("see_made")
        adj_turned = sem("adj_turned")
        turned_read = sem("turned_read")
        masks_step = sem("masks_step")
        edges_made = sem("edges_made")
        masks_made = sem("masks_made")
        see_ready = sem("see_ready")
        w_turned = sem("w_turned")
        w_ready = sem("w_ready")
        passed = sem("passed")
        scores_done = sem("scores_done")
        exp_done = sem("exp_done")
        probs_ready = sem("probs_ready")
        context_done = sem("context_done")
        context_read = sem("context_read")
        sums_done = sem("sums_done")
        sums_read = sem("sums_read")
        work_done = [sem(f"work_done{b}") for b in (0, 1)]
        work_read = [sem(f"work_read{b}") for b in (0, 1)]
        high_ready = sem("high_ready")
        gathered_step = sem("gathered_step")
        res_ready = sem("res_ready")
        y_summed = sem("y_summed")
        gamma_done = sem("gamma_done")
        x1_ready = sem("x1_ready")
        stats_done = {s: sem(f"{s}_stats_done") for s in norm}
        moments_done = {s: sem(f"{s}_moments_done") for s in norm}
        spread_done = {s: sem(f"{s}_spread_done") for s in norm}
        rstd_done = {s: sem(f"{s}_rstd_done") for s in norm}
        shift_done = {s: sem(f"{s}_shift_done") for s in norm}
        normed = {s: sem(f"{s}_normed") for s in norm}
        peak_step = sem("peak_step")
        peak_done = sem("peak_done")
        leaky_done = sem("leaky_done")
        hidden_done = sem("hidden_done")
        gat_exp_done = sem("gat_exp_done")
        gat_done = sem("gat_done")
        gat_read = sem("gat_read")
        divided = sem("divided")
        negative_ready = sem("negative_ready")
        negative_exp = sem("negative_exp")
        elu_step = sem("elu_step")
        out_ready = sem("out_ready")

        def wait(engine, semaphore, value):
            if not isinstance(value, int) or value > 0:
                engine.wait_ge(semaphore, value)

        def stand_alone(engine):
            engine.sem_inc(passed, 1)

        def adj_raw(t):
            home = context if t < 4 else probs[:, 0] if t < 6 else probs[:, 1]
            at = t if t < 4 else (t - 4) % 2
            return home[:, 2 * at:2 * at + 2, :].rearrange("p a n -> p (a n)").bitcast(I32)

        def bf16_slot(s):
            return ring[:, s, :].bitcast(BF16)

        def adj_bf16(t):
            return bf16_slot(t % 2)

        def turned_bf16(t):
            return bf16_slot(4 + t % 2)

        def edges_bf16(t):
            return bf16_slot(6 + t % 2)

        def adj_turned_ps(t):
            return score[:, t % SCORES, :].bitcast(BF16)

        def mask_step(i, q, c, j):
            if i.register is None and i.offset == FIRST and (q, c, j) in MASKS_AT:
                return MASKS_AT.index((q, c, j))
            return None

        def ring_tiles(s):
            return ring[:, s, :].rearrange("p (t f) -> p t f", t=TILES)

        block = ctx.enter_context(nc.Block())

        @block.sync
        def _(sp):
            for q in (0, 1):
                sp.dma_start(x_in[:, q], x_half[q]).then_inc(x_loaded, 16)
            for t in range(CHUNKS):
                sp.dma_start(adj_raw(t), adj_tile[t]).then_inc(adj_loaded[t], 16)
            def alone(semaphore, value):
                wait(sp, semaphore, value)
                if not isinstance(value, int):
                    stand_alone(sp)

            def stack(to, parts, picks, q, done):
                for h in range(HEADS):
                    for s, part in enumerate(picks):
                        sp.dma_start(to[s * DH:(s + 1) * DH, h, q * HALF:(q + 1) * HALF].bitcast(F32),
                                     parts[h * DH:(h + 1) * DH, part, :].bitcast(F32)).then_inc(done, 16)

            def half_of(tensor, b, q):
                row = b.times(2, q)
                if isinstance(row, int):
                    return tensor[row]
                return tensor[bass.ds(row, 1)].rearrange("o p t f -> (o p) t f")

            def iteration(i):
                for q in (0, 1):
                    f = i + -1
                    for c in range(CHUNKS):
                        if c == 0 and f.live():
                            if f.register is not None or f.offset > 0 or q:
                                turned, at = ("turn_hidden1", i + -1) if q == 0 else ("turn_hidden0", i)
                                alone(work_done[bank_of(turned)], count(turned, at))
                                alone(x1_stored, f.times(32, 16 * q))
                            alone(h_stored, f.times(32, 16 * (q + 1)))
                            sp.dma_start(res[:, :, :], half_of(h_kept, f, q)).then_inc(res_loaded, 16)
                            sp.dma_start(h1[:, :, :], half_of(x_half, f, q)).then_inc(res_loaded, 16)
                        g, half = ((i + -3), 1) if q == 0 else ((i + -2), 0)
                        if c == (3 if q == 0 else 6) and g.live():
                            alone(work_done[bank_of(f"gat_turn{half}")], count(f"gat_turn{half}", i))
                            alone(x1_stored, g.times(32, 16 * (half + 1)))
                            sp.dma_start(ring_tiles(TURN), half_of(x1_kept, g, half)).then_inc(x1_loaded, 16)
                        if (q, c) == (0, 3) and i.live():
                            alone(work_read[bank_of("query1")], count("query1", i))
                            alone(scores_done, i.times(STEPS * HEADS))
                            stack(query_stack, query_parts, (0, 1, 0, 1), 1, queries_stacked)
                        if (q, c) == (1, 1) and (i + 1).live():
                            alone(work_read[bank_of("query0")], count("query0", i))
                            alone(scores_done, slot((i, 0, 7), 3, 1))
                            stack(query_stack, query_parts, (0, 1, 0, 1), 0, queries_stacked)
                        if (q, c) == (1, 2) and (i + 1).live():
                            alone(work_read[bank_of("key0")], count("key0", i))
                            alone(scores_done, slot((i, 1, 3), 3, 1))
                            stack(key_stack, key_parts, (0, 0, 1, 1), 0, keys_stacked)
                        if q == 0 and c in (4, 5) and (i + 1).live():
                            alone(normed[f"x{c - 4}"], (i + 1).times(1, 1))
                            sp.dma_start(half_of(h_kept, i + 1, c - 4), x_in[:, c - 4]).then_inc(h_stored, 16)
                        if (q, c) == (1, 5) and (i + 2).live():
                            alone(work_done[bank_of("turn_x1")], count("turn_x1", i))
                            alone(h_stored, (i + 2).times(32))
                            for half in (0, 1):
                                sp.dma_start(x_in[:, half], half_of(x_half, i + 2, half)).then_inc(x_loaded, 16)
                        if c == 6 and f.live():
                            alone(x1_ready, f.times(2, q + 1))
                            sp.dma_start(half_of(x1_kept, f, q), res[:, :, :]).then_inc(x1_stored, 16)
                        if (q, c) == (1, 6) and (i + 1).live():
                            alone(work_read[bank_of("key1")], count("key1", i))
                            alone(scores_done, slot((i, 1, 7), 3, 1))
                            stack(key_stack, key_parts, (0, 0, 1, 1), 1, keys_stacked)
                        if c == (5 if q == 0 else 7) and g.live():
                            alone(out_ready, g.times(2, half + 1))
                            sp.dma_start(half_of(out_half, g, half), ring_tiles(OUT_A)).then_inc(out_stored, 16)

            iterations(sp, iteration)
            sp.wait_ge(h_stored, 32 * BATCHES)
            sp.wait_ge(x1_stored, 32 * BATCHES)
            sp.wait_ge(out_stored, 32 * BATCHES)

        @block.gpsimd
        def _(pool):
            nc.gpsimd.memset(eye[:, :], 0.0).then_inc(consts_step, 1)
            nc.gpsimd.memset(not_eye[:, :], 1.0).then_inc(consts_step, 1)
            nc.gpsimd.memset(one_of[:, :, :], 0.0).then_inc(consts_step, 1)
            nc.gpsimd.memset(pick[:, :], 0.0).then_inc(consts_step, 1)
            nc.gpsimd.memset(ones[:, :], 1.0).then_inc(consts_made, 1)
            nc.gpsimd.memset(eps[:, :], EPS).then_inc(consts_made, 1)
            nc.gpsimd.memset(minus_half[:, :], -0.5).then_inc(consts_made, 1)
            pool.wait_ge(consts_step, 4)
            nc.gpsimd.affine_select(out=eye[:, :], in_=eye[:, :], compare_op=ALU.not_equal, fill=1.0, base=0,
                                    pattern=[[-1, P]], channel_multiplier=1).then_inc(consts_step, 1)
            nc.gpsimd.affine_select(out=not_eye[:, :], in_=not_eye[:, :], compare_op=ALU.not_equal, fill=0.0,
                                    base=0, pattern=[[-1, P]], channel_multiplier=1).then_inc(consts_made, 1)
            picked = one_of[:, :, :].rearrange("p c d -> p (c d)")[:, 0:CHUNKS * DH:DH + 1]
            nc.gpsimd.memset(picked, 1.0).then_inc(consts_made, 1)
            for g in range(HEADS):
                pool.wait_ge(consts_made, 5 + g)
                nc.gpsimd.memset(pick[g * DH:g * DH + 1, :], 1.0).then_inc(consts_made, 1)
            pool.wait_ge(consts_step, 5)
            pool.wait_ge(consts_made, 9)
            nc.gpsimd.tensor_copy(eye_b[:, :], eye[:, :]).then_inc(consts_made, 1)
            pool.wait_ge(w_loaded, 16 * 13)
            pool.wait_ge(consts_made, 10)

            def rstd(s, n):
                _, moments, spread, scale, _ = norm[s]
                pool.wait_ge(moments_done[s], n)
                nc.gpsimd.tensor_tensor(spread[:, :], moments[:, :, 1], eps[:, :], ALU.add).then_inc(spread_done[s], 1)
                pool.wait_ge(spread_done[s], n)
                nc.gpsimd.tensor_tensor(scale[:, :], spread[:, :], minus_half[:, :], ALU.pow
                                        ).then_inc(rstd_done[s], 1)

            def hide(g, n):
                half, j = n // CHUNKS, n % CHUNKS
                pool.wait_ge(leaky_done, g.times(2 * CHUNKS, n + 1))
                nc.gpsimd.tensor_tensor(ring[:, n % RING, :], ring[:, n % RING, :],
                                        see_t[:, j, half * HALF:(half + 1) * HALF], ALU.add).then_inc(hidden_done, 1)

            def at(i, q, c, j):
                f = i + -1
                if f.live():
                    if (c, j) == (1, 0):
                        pool.wait_ge(res_loaded, f.times(64, 32 * (q + 1)))
                        nc.gpsimd.tensor_tensor(res[:, :, :], res[:, :, :],
                                                rows[:, 1:2, :].broadcast_to([P, TILES, D]), ALU.add
                                                ).then_inc(res_ready, 1)
                    if (c, j) == (1, 1):
                        nc.gpsimd.tensor_tensor(h1[:, :, :], h1[:, :, :],
                                                rows[:, 3:4, :].broadcast_to([P, TILES, D]), ALU.add
                                                ).then_inc(res_ready, 1)
                    if (c, j) == (2, 3):
                        rstd("y", f.times(2, q + 1))
                    if (c, j) == (4, 0):
                        pool.wait_ge(normed["y"], f.times(2, q + 1))
                        nc.gpsimd.tensor_tensor(res[:, :, :], res[:, :, :],
                                                rows[:, 2:3, :].broadcast_to([P, TILES, D]), ALU.mult
                                                ).then_inc(gamma_done, 1)
                        pool.wait_ge(gamma_done, f.times(2, q + 1))
                        pool.wait_ge(res_ready, f.times(4, 2 * q + 2))
                        nc.gpsimd.tensor_tensor(res[:, :, :], res[:, :, :], h1[:, :, :], ALU.add
                                                ).then_inc(x1_ready, 1)
                    if (c, j) == (5, 2):
                        rstd("z", f.times(2, q + 1))
                if q == 0 and (i + 1).live():
                    if (c, j) == (0, 3):
                        rstd("x0", (i + 1).times(1, 1))
                    if (c, j) == (2, 0):
                        rstd("x1", (i + 1).times(1, 1))
                if (i + (q - 1)).live() and c and j == 2:
                    pool.wait_ge(work_read[bank_of(f"gather{q}{c}")], count(f"gather{q}{c}", i))
                    nc.gpsimd.tensor_tensor(gathered[:, :, :], gathered[:, :, :], scaled[:, :, :], ALU.add
                                            ).then_inc(gathered_step, 1)
                g = i + -2
                if g.live() and j in (0, 2):
                    _, q0, c0, j0 = moved(i, q, c, j, -1)
                    n = 0 if (q0, c0) == (0, 7) else 2 * c0 + 2 if q0 and c0 < 7 else None
                    if n == 0 and j0 == 1 and g.register is None and g.offset == 0:
                        pool.wait_ge(see_ready, 2 * CHUNKS)
                    if n is not None:
                        hide(g, n + j0 // 2)
                if mask_step(i, q, c, j) == CHUNKS:
                    pool.wait_ge(masks_made, CHUNKS)
                    pool.wait_ge(see_made, CHUNKS)
                    for t in range(CHUNKS):
                        for m in (see, see_t):
                            spot = m[:, t, t * P:(t + 1) * P]
                            nc.gpsimd.tensor_tensor(spot, spot, not_eye[:, :], ALU.mult).then_inc(see_ready, 1)

            def iteration(i):
                for q in (0, 1):
                    for c in range(CHUNKS):
                        for j in range(HEADS):
                            at(i, q, c, j)

            iterations(pool, iteration)

        @block.scalar
        def _(act):
            for n, w in enumerate((Wq, Wk, Wv, Wo)):
                act.dma_start(w_in[:, n, :], w).then_inc(w_loaded, 16)
            act.dma_start(w1[:, :], W).then_inc(w_loaded, 16)
            for e in (0, 1):
                act.dma_start(a_in[:, e:e + 1], a[e * D:(e + 1) * D, :]).then_inc(w_loaded, 16)
            for n, b in enumerate((bq, bk)):
                act.dma_start(bias_col[:, n:n + 1], b.rearrange("(f o) -> f o", o=1)).then_inc(w_loaded, 16)
            for n, b in enumerate((bv, bo, gamma, beta)):
                row = b.rearrange("(o f) -> o f", o=1).broadcast_to([P, D])
                act.dma_start(rows[:, n, :], row).then_inc(w_loaded, 16)
            act.wait_ge(w_turned, 1)
            nc.scalar.copy(w_t[:, :, :], ctx_ps[:, :].rearrange("p (t f) -> p t f", t=4)).then_inc(w_ready, 1)
            act.wait_ge(w_turned, 2)
            nc.scalar.copy(h1_t[:, 0:D], gat_ps[:, 0:D]).then_inc(w_ready, 1)
            act.wait_ge(w_turned, 3)
            nc.scalar.copy(w1_a[:, 0:2], sum_ps[:, 0:2]).then_inc(w_ready, 1)
            nc.scalar.mul(w1_a[:, 2:3], sum_ps[:, 1:2], 1 - SLOPE).then_inc(w_ready, 1)
            nc.scalar.mul(w1_a[:, 3:4], sum_ps[:, 1:2], SLOPE).then_inc(w_ready, 1)
            act.wait_ge(consts_made, 10)
            act.wait_ge(w_loaded, 16 * 13)

            def apply(s, n, to, source, function):
                _, _, _, scale, shift = norm[s]
                act.wait_ge(shift_done[s], n)
                for t in range(TILES):
                    last = nc.scalar.activation(to[:, t, :], source[:, t, :], function, bias=shift[:, t:t + 1],
                                                scale=scale[:, t:t + 1])
                last.then_inc(normed[s], 1)

            def gat_exp(g, n):
                act.wait_ge(hidden_done, g.times(2 * CHUNKS, n + 1))
                nc.scalar.activation(ring[:, n % RING, :], ring[:, n % RING, :], ACT.Exp,
                                     bias=ends[:, n % CHUNKS, 3:4]).then_inc(gat_exp_done, 1)

            def read_gat(g, half):
                act.wait_ge(gat_done, g.times(2, half + 1))
                act.wait_ge(work_done[bank_of(f"gat_sums{half}")], count(f"gat_sums{half}", g + 2 + half))
                wait(act, out_ready, g.times(2, half))
                nc.scalar.copy(ring[:, TURN, :], gat_ps[:, :]).then_inc(gat_read, 1)

            def negative_part(g, half):
                act.wait_ge(negative_ready, g.times(2, half + 1))
                nc.scalar.activation(ring[:, OUT_B, :], ring[:, OUT_B, :], ACT.Exp).then_inc(negative_exp, 1)

            def read_job(name, i, b):
                bank = bank_of(name)
                half = int(name[-1])
                side = slice(half * HALF, (half + 1) * HALF)
                act.wait_ge(work_done[bank], count(name, i))
                if name.startswith("query") or name.startswith("key"):
                    is_key = name.startswith("key")
                    parts = key_parts if is_key else query_parts
                    wait(act, keys_stacked if is_key else queries_stacked, b.times(512, 256 * half))
                    nc.scalar.activation(parts[:, 0, :], work[:, bank, :], ACT.Identity,
                                         bias=bias_col[:, int(is_key):int(is_key) + 1]).then_inc(high_ready, 1)
                    return
                if name.startswith("turn_context"):
                    to = context_t[:, :]
                elif name.startswith("turn_hidden"):
                    to = h1_t[:, side]
                elif name.startswith("turn_x"):
                    to = h_t[:, side]
                elif name.startswith("wh"):
                    to = wh[:, half * TILES:(half + 1) * TILES, :].rearrange("p t f -> p (t f)")
                elif name.startswith("to_row"):
                    wait(act, leaky_done, b.times(2 * CHUNKS))
                    to = to_row[:, side]
                elif name.startswith("base_row"):
                    to = to_row[:, side]
                elif name.startswith("near_row"):
                    to = near_row[:, side]
                else:
                    assert name.startswith("gat_sums"), name
                    to = ring[:, SUMS, :]
                nc.scalar.copy(to, work[:, bank, :]).then_inc(work_read[bank], 1)

            def at(i, q, c, j):
                t = mask_step(i, q, c, j)
                if t is not None and t < CHUNKS:
                    act.wait_ge(adj_loaded[t], 16)
                    if t >= 2:
                        act.wait_ge(adj_turned, t - 1)
                        act.wait_ge(see_made, t - 1)
                    nc.scalar.copy(adj_bf16(t), adj_raw(t)).then_inc(adj_cast, 1)
                if t:
                    act.wait_ge(adj_turned, t)
                    if t >= 3:
                        act.wait_ge(edges_made, t - 2)
                    nc.scalar.copy(turned_bf16(t - 1), adj_turned_ps(t - 1)).then_inc(turned_read, 1)
                step, h = ahead(i, q, c, j, 5)
                if step[0].live():
                    bank, _ = score_bank(step, h)
                    act.wait_ge(scores_done, slot(step, h, 1))
                    nc.scalar.activation(score[:, bank, :], score[:, bank, :], ACT.Exp, scale=DH ** -0.5
                                         ).then_inc(exp_done, 1)
                if j == 3 and i.live():
                    act.wait_ge(context_done, number((i, q, c), 1))
                    if (i + (q - 1)).live():
                        act.wait_ge(work_done[bank_of(f"gather{q}{c}")], count(f"gather{q}{c}", i))
                    nc.scalar.copy(context[:, c, :], ctx_ps[:, :]).then_inc(context_read, 1)
                if j == 3 and c == CHUNKS - 1 and i.live():
                    act.wait_ge(sums_done, number((i, q, c), 1))
                    nc.scalar.copy(sums[:, :], sum_ps[:, :]).then_inc(sums_read, 1)
                i_job, *place = moved(i, q, c, j, -1)
                name, off = JOB_AT.get(tuple(place), (None, 0))
                if name and (i_job + off).live() and not name.startswith(READ_BY_VECTOR):
                    read_job(name, i_job, i_job + off)
                f = i + -1
                if f.live():
                    n = f.times(2, q + 1)
                    if (c, j) == (3, 3):
                        apply("y", n, res, res, ACT.Identity)
                    if (c, j) == (6, 2):
                        apply("z", n, h1, res, ACT.Relu)
                if q == 0 and (i + 1).live():
                    for half, at_apply in enumerate(((2, 1), (3, 1))):
                        n = (i + 1).times(1, 1)
                        if (c, j) == at_apply:
                            apply(f"x{half}", n, x_in[:, half], x_in[:, half], ACT.Relu)
                g = i + -2
                if g.live():
                    if q and j in (1, 3):
                        gat_exp(g, 2 * c + j // 2)
                    if (q, c, j) == (1, 5, 1):
                        read_gat(g, 0)
                    if (q, c, j) == (1, 6, 3):
                        negative_part(g, 0)
                g = i + -3
                if g.live():
                    if (q, c, j) == (0, 1, 3):
                        read_gat(g, 1)
                    if (q, c, j) == (0, 4, 1):
                        negative_part(g, 1)

            def iteration(i):
                for q in (0, 1):
                    for c in range(CHUNKS):
                        for j in range(HEADS):
                            at(i, q, c, j)

            iterations(act, iteration)

        @block.vector
        def _(dve):
            dve.wait_ge(w_loaded, 16 * 13)

            def masks(t):
                if t < CHUNKS:
                    dve.wait_ge(adj_cast, t + 1)
                    nc.vector.tensor_scalar(see[:, t, :], adj_bf16(t), 0.0, OUT_OF_SIGHT, ALU.is_le, ALU.mult
                                            ).then_inc(see_made, 1)
                if t:
                    dve.wait_ge(turned_read, t)
                    nc.vector.tensor_scalar(edges_bf16(t - 1), turned_bf16(t - 1), 0.0, None, ALU.not_equal
                                            ).then_inc(masks_step, 1)
                    columns = slice((t - 1) * P, t * P)
                    nc.vector.tensor_scalar(see_t[:, :, columns],
                                            turned_bf16(t - 1).rearrange("p (j i) -> p j i", i=P), 0.0,
                                            OUT_OF_SIGHT, ALU.is_le, ALU.mult).then_inc(edges_made, 1)
                    dve.wait_ge(masks_step, t)
                    nc.vector.tensor_scalar(cap[:, :, columns],
                                            edges_bf16(t - 1).rearrange("p (j i) -> p j i", i=P), HIGH, LOW,
                                            ALU.mult, ALU.max).then_inc(masks_made, 1)

            def moments(s, n, source):
                stats, moment, _, _, _ = norm[s]
                for t in range(TILES):
                    last = nc.vector.bn_stats(stats[:, t, :], source[:, t, :])
                last.then_inc(stats_done[s], 1)
                dve.wait_ge(stats_done[s], n)
                stand_alone(dve)
                for t in range(TILES):
                    last = nc.vector.bn_aggr(moment[:, t, :], stats[:, t, :])
                last.then_inc(moments_done[s], 1)

            def shift(s, n):
                _, moment, _, scale, to = norm[s]
                dve.wait_ge(rstd_done[s], n)
                nc.vector.scalar_tensor_tensor(out=to[:, :], in0=moment[:, :, 0], scalar=-1.0, in1=scale[:, :],
                                               op0=ALU.mult, op1=ALU.mult).then_inc(shift_done[s], 1)

            def heads(tile):
                return tile.rearrange("p t (h d) -> p t h d", h=HEADS)

            def gather(i, name, b, q, chunk):
                to = gathered if chunk == 0 else scaled
                if chunk == 0:
                    sums_job = f"turn_sums{1 - q}"
                    dve.wait_ge(work_read[bank_of(sums_job)], count(sums_job, i))
                wait(dve, gathered_step, b.times(14, 7 * q + max(chunk - 1, 0)))
                dve.wait_ge(work_done[bank_of(name)], count(name, i))
                share = inverse[:, :, :, chunk:chunk + 1].broadcast_to([P, TILES, HEADS, DH])
                nc.vector.tensor_tensor(heads(to[:, :, :]), heads(in_tiles(bank_of(name))), share, ALU.mult
                                        ).then_inc(work_read[bank_of(name)], 1)

            def see_peak(g, t):
                if t:
                    dve.wait_ge(peak_step, g.times(PEAK_STEPS, t))
                    stand_alone(dve)
                nc.vector.tensor_tensor_reduce(
                    out=ring[:, RING - 2:RING, :].rearrange("p a n -> p (a n)"), in0=to_row[:, :], in1=see[:, t, :],
                    scale=1.0, scalar=-3e38, op0=ALU.add, op1=ALU.max, accum_out=peak[:, t:t + 1]
                ).then_inc(peak_step, 1)

            def shifts(g):
                dve.wait_ge(peak_step, g.times(PEAK_STEPS, CHUNKS))
                nc.vector.tensor_tensor(peak[:, :], peak[:, :], ends[:, :, 0], ALU.add).then_inc(peak_step, 1)
                dve.wait_ge(peak_step, g.times(PEAK_STEPS, CHUNKS + 1))
                nc.vector.tensor_scalar(peak[:, :], peak[:, :], -1.0, None, ALU.mult).then_inc(peak_step, 1)
                dve.wait_ge(peak_step, g.times(PEAK_STEPS, CHUNKS + 2))
                nc.vector.scalar_tensor_tensor(out=peak[:, :], in0=peak[:, :], scalar=SLOPE, in1=peak[:, :],
                                               op0=ALU.mult, op1=ALU.min).then_inc(peak_step, 1)
                dve.wait_ge(peak_step, g.times(PEAK_STEPS, CHUNKS + 3))
                for n, part in enumerate((1.0, SLOPE)):
                    nc.vector.scalar_tensor_tensor(out=row_shift[:, n, :], in0=ends[:, :, 0], scalar=part,
                                                   in1=peak[:, :], op0=ALU.mult, op1=ALU.add).then_inc(peak_done, 1)

            def leaky(g, n, i):
                half, j = n // CHUNKS, n % CHUNKS
                if n % CHUNKS == 0:
                    dve.wait_ge(work_read[bank_of(f"base_row{half}")], count(f"base_row{half}", i))
                if n == TURN:
                    wait(dve, out_stored, g.times(32))
                if n == RING:
                    dve.wait_ge(work_done[bank_of("gat_sums0")], count("gat_sums0", i))
                side = slice(half * HALF, (half + 1) * HALF)
                nc.vector.scalar_tensor_tensor(out=ring[:, n % RING, :], in0=near_row[:, side],
                                               scalar=ends[:, j, 2:3], in1=to_row[:, side],
                                               op0=ALU.add, op1=ALU.max).then_inc(leaky_done, 1)

            def divide_gat(i, g, half):
                name = f"gat_turn{half}"
                bank = bank_of(name)
                sums_job = f"gat_turn_sums{half}"
                dve.wait_ge(work_read[bank_of(sums_job)], count(sums_job, i))
                dve.wait_ge(work_done[bank], count(name, i))
                wait(dve, out_stored, g.times(32, 16 * half))
                nc.vector.tensor_tensor(ring_tiles(OUT_A), in_tiles(bank),
                                        gat_inverse[:, :].unsqueeze(2).broadcast_to([P, TILES, D]), ALU.mult
                                        ).then_inc(work_read[bank], 1)
                dve.wait_ge(work_read[bank], count(name, i))
                nc.vector.tensor_scalar(ring[:, OUT_B, :], ring[:, OUT_A, :], 0.0, None, ALU.min
                                        ).then_inc(negative_ready, 1)

            def elu(g, half):
                dve.wait_ge(negative_exp, g.times(2, half + 1))
                nc.vector.scalar_tensor_tensor(out=ring[:, OUT_B, :], in0=ring[:, OUT_A, :], scalar=0.0,
                                               in1=ring[:, OUT_B, :], op0=ALU.max, op1=ALU.add).then_inc(elu_step, 1)
                dve.wait_ge(x1_loaded, g.times(32, 16 * (half + 1)))
                dve.wait_ge(elu_step, g.times(2, half + 1))
                nc.vector.scalar_tensor_tensor(out=ring[:, OUT_A, :], in0=ring[:, OUT_B, :], scalar=-1.0,
                                               in1=ring[:, TURN, :], op0=ALU.add, op1=ALU.add).then_inc(out_ready, 1)

            def read_job(name, i, b):
                bank = bank_of(name)
                digits = [int(d) for d in name if d.isdigit()]
                if name.startswith("query") or name.startswith("key"):
                    is_key = name.startswith("key")
                    parts = key_parts if is_key else query_parts
                    turn = {"query0": 1, "key0": 2, "key1": 3, "query1": 4}[name]
                    dve.wait_ge(high_ready, b.times(4, turn))
                    nc.vector.scalar_tensor_tensor(
                        out=parts[:, 1, :], in0=work[:, bank, :], scalar=bias_col[:, int(is_key):int(is_key) + 1],
                        in1=parts[:, 0, :].bitcast(F32), op0=ALU.add, op1=ALU.subtract
                    ).then_inc(work_read[bank], 1)
                    return
                if name.startswith("gather"):
                    gather(i, name, b, 1 - digits[0], digits[1])
                    return
                if name.startswith("gat_turn") and not name.startswith("gat_turn_sums"):
                    divide_gat(i, b, digits[0])
                    return
                dve.wait_ge(work_done[bank], count(name, i))
                if name.startswith("turn_sums"):
                    found = work[:, bank, :].rearrange("p (t h r) -> p t h r", t=TILES, h=HEADS)
                    nc.vector.reciprocal(inverse[:, :, :, :], found[:, :, :, 0:CHUNKS]).then_inc(work_read[bank], 1)
                elif name.startswith("value"):
                    half = digits[0]
                    nc.vector.tensor_tensor(value[:, half * TILES:(half + 1) * TILES, :], in_tiles(bank),
                                            rows[:, 0:1, :].broadcast_to([P, TILES, D]), ALU.add
                                            ).then_inc(work_read[bank], 1)
                elif name.startswith("project"):
                    q = digits[0]
                    dve.wait_ge(res_ready, b.times(4, 2 * q + 1))
                    nc.vector.tensor_tensor(res[:, :, :], in_tiles(bank), res[:, :, :], ALU.add
                                            ).then_inc(work_read[bank], 1)
                    dve.wait_ge(work_read[bank], count(name, i))
                    moments("y", b.times(2, q + 1), res)
                elif name == "ends":
                    nc.vector.tensor_copy(ends[:, :, :].rearrange("p t e -> p (t e)"), work[:, bank, 0:4 * CHUNKS]
                                          ).then_inc(work_read[bank], 1)
                else:
                    assert name.startswith("gat_turn_sums"), name
                    nc.vector.reciprocal(gat_inverse[:, :], work[:, bank, 0:TILES]).then_inc(work_read[bank], 1)

            def at(i, q, c, j):
                t = mask_step(i, q, c, j)
                if t is not None:
                    masks(t)
                step, h = ahead(i, q, c, j, 4)
                if step[0].live():
                    if h == 0:
                        wait(dve, sums_done, number(step, -1))
                        if step[0].register is None and step[0].offset == 0 and step[1:] == (0, 0):
                            dve.wait_ge(masks_made, CHUNKS)
                    dve.wait_ge(exp_done, slot(step, h, 1))
                    nc.vector.scalar_tensor_tensor(
                        out=probs[:, step[2] % 2, h, :], in0=score[:, score_bank(step, h)[0], :], scalar=LOW,
                        in1=cap[:, step[2], step[1] * HALF:(step[1] + 1) * HALF],
                        op0=ALU.max, op1=ALU.min).then_inc(probs_ready, 1)
                for back in (2, 1):
                    i_job, *place = moved(i, q, c, j, -back)
                    name, off = JOB_AT.get(tuple(place), (None, 0))
                    if name and (i_job + off).live() and name.startswith(
                            READ_BY_VECTOR if back == 1 else ("query", "key")):
                        read_job(name, i_job, i_job + off)
                f = i + -1
                if f.live():
                    n = f.times(2, q + 1)
                    if (c, j) == (3, 1):
                        shift("y", n)
                    if (c, j) == (5, 1):
                        dve.wait_ge(x1_ready, n)
                        moments("z", n, res)
                    if (c, j) == (6, 0):
                        shift("z", n)
                if q == 0 and (i + 1).live():
                    for half, (c0, j0, c1, j1) in enumerate(((0, 2, 1, 2), (1, 1, 2, 3))):
                        n = (i + 1).times(1, 1)
                        if (c, j) == (c0, j0):
                            dve.wait_ge(x_loaded, (i + 1).times(32, 32))
                            moments(f"x{half}", n, x_in[:, half])
                        if (c, j) == (c1, j1):
                            shift(f"x{half}", n)
                g = i + -2
                if g.live():
                    if q == 0 and (c, j) in PEAKS_AT:
                        t = PEAKS_AT.index((c, j))
                        if t == 0:
                            if g.register is None and g.offset == 0:
                                dve.wait_ge(see_ready, 2 * CHUNKS)
                            dve.wait_ge(work_read[bank_of("ends")], count("ends", i))
                            stand_alone(dve)
                        see_peak(g, t)
                        if t == CHUNKS - 1:
                            shifts(g)
                    n = 0 if (q, c) == (0, 7) else 2 * c + 2 if q and c < 7 else None
                    if n is not None and j in (1, 3):
                        leaky(g, n + j // 2, i)
                    if (q, c, j) == (1, 7, 2):
                        elu(g, 0)
                g = i + -3
                if g.live() and (q, c, j) == (0, 5, 2):
                    elu(g, 1)

            def iteration(i):
                for q in (0, 1):
                    for c in range(CHUNKS):
                        for j in range(HEADS):
                            at(i, q, c, j)

            iterations(dve, iteration)

        @block.tensor
        def _(pe):
            pe.wait_ge(w_loaded, 16 * 13)
            pe.wait_ge(consts_made, 10)
            for n in range(4):
                last = nc.tensor.transpose(ctx_ps[:, n * D:(n + 1) * D], w_in[:, n, :], eye[:, :])
            last.then_inc(w_turned, 1)
            nc.tensor.transpose(gat_ps[:, 0:D], w1[:, :], eye[:, :]).then_inc(w_turned, 1)
            pe.wait_ge(w_ready, 2)
            nc.tensor.matmul(sum_ps[:, 0:2], h1_t[:, 0:D], a_in[:, :], start=True, stop=True).then_inc(w_turned, 1)
            pe.wait_ge(w_ready, 5)

            def turn(bank, source):
                for t in range(TILES):
                    last = nc.tensor.transpose(work[:, bank, t * P:(t + 1) * P], source(t), eye[:, :])
                return last

            def product(bank, pairs):
                for t, (left, right) in enumerate(pairs):
                    last = nc.tensor.matmul(work[:, bank, t * P:(t + 1) * P], left, right, start=True, stop=True)
                return last

            def wait_read(name, i):
                wait(pe, work_read[bank_of(name)], count(name, i))

            def job(i, name, b, q, c):
                bank = bank_of(name)
                wait(pe, work_read[bank], count(name, i) + -1)
                half = int(name[-1]) if name[-1].isdigit() else 0
                side = slice(half * HALF, (half + 1) * HALF)
                if name.startswith("gather"):
                    pe.wait_ge(context_read, number((b, 1 - q, c), 1))
                    last = turn(bank, lambda t: context[:, c, t * P:(t + 1) * P])
                elif name.startswith("turn_sums"):
                    pe.wait_ge(sums_read, b.times(2, (1 - q) + 1))
                    last = turn(bank, lambda t: sums[:, t * P:(t + 1) * P])
                elif name.startswith("turn_context"):
                    pe.wait_ge(gathered_step, b.times(14, 7 * (q + 1)))
                    last = turn(bank, lambda t: gathered[:, t, :])
                elif name.startswith("project"):
                    wait_read(f"turn_context{q}", i)
                    last = product(bank, [(context_t[:, t * P:(t + 1) * P], w_t[:, 3, :]) for t in range(TILES)])
                elif name.startswith("turn_hidden"):
                    pe.wait_ge(normed["z"], b.times(2, q + 1))
                    last = turn(bank, lambda t: h1[:, t, :])
                elif name.startswith("turn_x"):
                    pe.wait_ge(normed[f"x{half}"], b.times(1, 1))
                    last = turn(bank, lambda t: x_in[:, half, t, :])
                elif name.startswith("query"):
                    if half == 0:
                        wait_read("turn_x1", i)
                    last = nc.tensor.matmul(work[:, bank, :], w_t[:, 0, :], h_t[:, side], start=True, stop=True)
                elif name.startswith("key"):
                    last = nc.tensor.matmul(work[:, bank, :], w_t[:, 1, :], h_t[:, side], start=True, stop=True)
                elif name.startswith("value"):
                    last = product(bank, [(h_t[:, (half * TILES + t) * P:(half * TILES + t + 1) * P], w_t[:, 2, :])
                                    for t in range(TILES)])
                elif name.startswith("wh"):
                    last = product(bank, [(h1_t[:, (half * TILES + t) * P:(half * TILES + t + 1) * P], w1[:, :])
                                    for t in range(TILES)])
                elif name == "ends":
                    for t in range(CHUNKS):
                        last = nc.tensor.matmul(work[:, bank, 4 * t:4 * t + 4], h1_t[:, t * P:(t + 1) * P], w1_a[:, :],
                                                start=True, stop=True)
                elif name.startswith("to_row"):
                    if half == 0:
                        wait_read("turn_hidden1", i + -1)
                    last = nc.tensor.matmul(work[:, bank, :], w1_a[:, 1:2].broadcast_to([P, P]), h1_t[:, side],
                                            start=True, stop=True)
                elif name.startswith("near_row") or name.startswith("base_row"):
                    pe.wait_ge(peak_done, b.times(2, 2))
                    kind = int(name.startswith("base"))
                    last = product(bank, [(row_shift[:, kind, half * TILES + t:half * TILES + t + 1].broadcast_to([P, P]),
                                     eye[:, :]) for t in range(TILES)])
                elif name.startswith("gat_sums"):
                    for jt in range(CHUNKS):
                        g = jt % 4
                        last = nc.tensor.matmul(work[g * DH:(g + 1) * DH, bank, :], ones[:, :],
                                                ring[:, (half * CHUNKS + jt) % RING, :],
                                                start=jt < 4, stop=jt >= 4)
                elif name.startswith("gat_turn_sums"):
                    wait_read(f"gat_sums{half}", i)
                    for t in range(TILES):
                        last = nc.tensor.matmul(work[:, bank, t:t + 1], ring[:, SUMS, t * P:(t + 1) * P], pick[:, :],
                                                start=True, stop=True)
                else:
                    assert name.startswith("gat_turn"), name
                    pe.wait_ge(gat_read, b.times(2, half + 1))
                    last = turn(bank, lambda t: ring[:, TURN, t * P:(t + 1) * P])
                last.then_inc(work_done[bank], 1)

            def neighbours(g, n):
                half, jt = n // CHUNKS, n % CHUNKS
                pe.wait_ge(gat_exp_done, g.times(2 * CHUNKS, n + 1))
                if jt == 0:
                    wait(pe, gat_read, g.times(2, half))
                last = nc.tensor.matmul(gat_ps[:, :], wh[:, jt, :], ring[:, n % RING, :], start=jt == 0,
                                        stop=jt == CHUNKS - 1)
                if jt == CHUNKS - 1:
                    last.then_inc(gat_done, 1)

            def at(i, q, c, j):
                t = mask_step(i, q, c, j)
                if t is not None and t < CHUNKS:
                    pe.wait_ge(adj_cast, t + 1)
                    if t >= SCORES:
                        pe.wait_ge(turned_read, t - SCORES + 1)
                    for jt in range(CHUNKS):
                        last = nc.tensor.transpose(adj_turned_ps(t)[:, jt * P:(jt + 1) * P],
                                                   adj_bf16(t)[:, jt * P:(jt + 1) * P], eye_b[:, :])
                    last.then_inc(adj_turned, 1)
                step, h = ahead(i, q, c, j, 6)
                if step[0].live():
                    b, sq, sc = step
                    if h == 0 and sc == 0:
                        pe.wait_ge(queries_stacked, b.times(512, 256 * (sq + 1)))
                    if h == 0 and sq == 0 and sc in (0, TILES):
                        pe.wait_ge(keys_stacked, b.times(512, 256 * (sc // TILES + 1)))
                    if b.register is None and b.offset == 0 and (sq, sc, h) == (0, 0, 0):
                        pe.wait_ge(turned_read, CHUNKS)
                    bank, back = score_bank(step, h)
                    wait(pe, probs_ready, slot(step, h, 1 - back))
                    nc.tensor.matmul(score[:, bank, :], key_stack[:, h, sc * P:(sc + 1) * P],
                                     query_stack[:, h, sq * HALF:(sq + 1) * HALF], start=True, stop=True
                                     ).then_inc(scores_done, 1)
                if i.live() and j == 1:
                    if (q, c) == (0, 0):
                        wait_read("value0", i + -1)
                    if (q, c) == (0, TILES):
                        wait_read("value1", i)
                    pe.wait_ge(probs_ready, slot((i, q, c), HEADS))
                    wait(pe, context_read, number((i, q, c)))
                    for h in range(HEADS):
                        last = nc.tensor.matmul(ctx_ps[h * DH:(h + 1) * DH, :], value[:, c, h * DH:(h + 1) * DH],
                                                probs[:, c % 2, h, :], start=True, stop=True)
                    last.then_inc(context_done, 1)
                if i.live() and j == 2:
                    if c == 0:
                        wait(pe, sums_read, i.times(2, q))
                    for h in range(HEADS):
                        last = nc.tensor.matmul(sum_ps[h * DH:(h + 1) * DH, :], one_of[:, c, :],
                                                probs[:, c % 2, h, :], start=c == 0, stop=c == CHUNKS - 1)
                    last.then_inc(sums_done, 1)
                name, off = JOB_AT.get((q, c, j), (None, 0))
                if name and (i + off).live():
                    job(i, name, i + off, q, c)
                if j in (0, 2):
                    if q and c and (i + -2).live():
                        neighbours(i + -2, 2 * c - 2 + j // 2)
                    if (q, c) == (0, 0) and (i + -3).live():
                        neighbours(i + -3, 2 * CHUNKS - 2 + j // 2)

            def iteration(i):
                for q in (0, 1):
                    for c in range(CHUNKS):
                        for j in range(HEADS):
                            at(i, q, c, j)

            iterations(pe, iteration)


_INS = ["x", "adj", "L0_gnn_Wq", "L0_gnn_bq", "L0_gnn_Wk", "L0_gnn_bk", "L0_gnn_Wv", "L0_gnn_bv", "L0_gnn_Wo",
        "L0_gnn_bo", "L0_gnn_gamma", "L0_gnn_beta", "L1_gnn_W", "L1_gnn_a"]


def kernel(**inputs):
    import numpy as np
    import concourse.bacc as bacc
    from concourse.bass_utils import run_bass_kernel_spmd

    nc = bacc.Bacc("TRN2", target_bir_lowering=False, num_devices=1)
    arrays, args = {}, []
    for name in _INS:
        array = np.ascontiguousarray(inputs[name])
        arrays[f"in_{name}"] = array
        args.append(nc.dram_tensor(f"in_{name}", array.shape, mybir.dt.from_np(array.dtype), kind="ExternalInput").ap())
    args.append(nc.dram_tensor("out_0", (BATCHES, N, D), F32, kind="ExternalOutput").ap())
    build(nc, *args)
    result = run_bass_kernel_spmd(nc, [arrays], core_ids=[0])
    return result.results[0]["out_0"]
```

```python
from contextlib import ExitStack

import concourse.bass as bass
from concourse import mybir

F32 = mybir.dt.float32
F32R = mybir.dt.float32r
BF16 = mybir.dt.bfloat16
I32 = mybir.dt.int32
ALU = mybir.AluOpType
ACT = mybir.ActivationFunctionType

P = 128
BATCHES, N, D = 8, 1024, 128
HEADS = 4
DH = D // HEADS
CHUNKS = N // P
HALF = N // 2
TILES = HALF // P
STEPS = 2 * CHUNKS
EPS = 1e-5
LOW, HIGH = 4.5399929762484854e-05, 22026.465794806718
OUT_OF_SIGHT = -1e30
SLOPE = 0.2
RING = 12
SCORES = 3
PEAK_STEPS = CHUNKS + 2
WIDE = D + 4
WH_TILES = {"wh0": range(0, 3), "wh1": range(3, 6), "wh2": range(6, CHUNKS)}
TURN, SUMS, OUT_A, OUT_B = 4, 5, 6, 7

SLOTS = STEPS * HEADS
PHASE = SLOTS // 2

PLACES = {
    "turn_sums0": (0, -1), "turn_context0": (1, -1), "to_row0": (3, -2), "project0": (5, -1),
    "to_row1": (7, -2), "value1": (13, 0), "turn_x0": (14, 1), "query1": (17, 0), "turn_x1": (19, 1),
    "wh2": (21, -2), "wh0": (22, -2), "wh1": (23, -2), "base_row0": (26, -2), "near_row0": (27, -2),
    "near_row1": (29, -2), "turn_hidden0": (30, -1), "base_row1": (31, -2), "turn_sums1": (32, 0),
    "turn_context1": (33, -1), "query0": (35, 1), "key0": (39, 1), "project1": (43, -1), "key1": (49, 1),
    "gat_sums0": (54, -2), "value0": (55, 1), "gat_turn_sums0": (57, -2), "gat_turn0": (61, -2),
    "turn_hidden1": (63, -1), "gat_sums1": (79, -2), "gat_turn_sums1": (82, -2), "gat_turn1": (89, -2),
}
GATHERS = [2, 4, 8, 12, 16, 20, 24, 28]
for _q in (0, 1):
    for _c, _slot in enumerate(GATHERS):
        PLACES[f"gather{_q}{_c}"] = (_slot + PHASE * _q, _q - 1)
READ_AFTER = {"query0": 2, "query1": 2, "key0": 2, "key1": 2, "turn_sums0": 2, "gat_sums0": 2, "near_row0": 2, "gat_turn_sums1": 2}
HIGH_AFTER, ADD_AFTER = 1, 1
SCORES_AHEAD, EXP_AHEAD, PROBS_AHEAD = 6, 5, 4
CONTEXT_AT, SUMS_AT, CONTEXT_READ_AT, SUMS_READ_AT = 1, 2, 3, 3
IN_PHASE = {
    "residual": 4, "beta": 6, "rstd_y": 11, "shift_y": 13, "apply_y": 15, "gamma": 16, "x1": 16,
    "moments_z": 22, "rstd_z": 22, "shift_z": 24, "apply_z": 25,
}
ONCE = {
    "moments_x0": 2, "rstd_x0": 3, "moments_x1": 5, "shift_x0": 7, "rstd_x1": 8, "apply_x0": 9, "shift_x1": 12,
    "apply_x1": 13, "read_gat0": 60, "negative0": 64, "add_residual0": 65, "add_negative0": 66,
    "read_gat1": 80, "negative1": 92, "add_residual1": 93, "add_negative1": 94,
}
PEAKS_AT = [10, 12, 14, 16, 18, 20, 22, 24]
LEAKY_AT = [29, 32, 34, 36, 39, 42, 44, 46, 50, 52, 55, 58, 60, 62, 65, 68]
HIDE_AT = [31, 34, 36, 39, 42, 45, 47, 48, 52, 54, 57, 60, 62, 62, 65, 68]
GAT_EXP_AT = [36, 39, 41, 43, 46, 49, 51, 53, 57, 59, 62, 65, 67, 69, 72, 75]
NEIGHBOURS_AT = [40, 43, 45, 47, 50, 53, 55, 57, 61, 63, 66, 69, 71, 73, 76, 79]
MASKS_AT = [29, 33, 36, 40, 45, 48, 49, 50, 54]
WEIGHTS_AT = 46
SYNC_IN_PHASE = {
    "load_residual": 0, "store_x1": 24,
}
SYNC_COMING = {
    "load_x": -12, "store_h0": 16, "store_h1": 20, "stack_query0": 36, "stack_key0": 40, "stack_key1": 56,
    "stack_query1": 76,
}
SYNC_SECOND = {
    "load_x1_0": 61, "store_out0": 67, "load_x1_1": 89, "store_out1": 97,
}

JOBS = sorted((slot % SLOTS, name, graph - slot // SLOTS) for name, (slot, graph) in PLACES.items())
JOB_AT = {slot: (name, graph) for slot, name, graph in JOBS}
ORDER = {name: n for n, (_, name, _) in enumerate(JOBS)}
OFFSET = {name: graph for _, name, graph in JOBS}
assert len(JOB_AT) == len(JOBS)
FIRST, LAST = -1, BATCHES + 2
LOOP = range(3, BATCHES - 2)
READ_BY_VECTOR = ("gather", "turn_sums", "project", "gat_turn")


class Graph:

    def __init__(self, offset, register=None):
        self.offset, self.register = offset, register

    def __add__(self, n):
        return Graph(self.offset + n, self.register)

    def live(self):
        return self.register is not None or 0 <= self.offset < BATCHES

    def times(self, k, plus=0):
        constant = self.offset * k + plus
        return constant if self.register is None else self.register * k + constant


def jobs_of(i, bank):
    return [n for n, (_, _, off) in enumerate(JOBS) if n % 2 == bank and 0 <= i + off < BATCHES]


def jobs_before(i, bank):
    return sum(len(jobs_of(k, bank)) for k in range(FIRST, i))


def bank_of(name):
    return ORDER[name] % 2


def count(name, i):
    n, bank = ORDER[name], bank_of(name)
    if i.register is None:
        return jobs_before(i.offset, bank) + sum(m <= n for m in jobs_of(i.offset, bank))
    everyone = range(bank, len(JOBS), 2)
    at = Graph(i.offset - LOOP[0], i.register)
    start = jobs_before(LOOP[0], bank) + n // 2 + 1
    for k in LOOP:
        assert count(name, Graph(k + i.offset)) == (k + at.offset) * len(everyone) + start, name
    return at.times(len(everyone), start)


def count_of(name, graph):
    return count(name, graph + -OFFSET[name])


def iterations(engine, body):
    for i in range(FIRST, LOOP[0]):
        body(Graph(i))
    with engine.Fori(LOOP[0], LOOP[-1] + 1) as register:
        body(Graph(0, register))
    for i in range(LOOP[-1] + 1, LAST + 1):
        body(Graph(i))


def moved(i, q, c, j, places):
    whole, n = divmod(slot_of(q, c, j) + places, SLOTS)
    return (i + whole if whole else i), n // PHASE, n % PHASE // HEADS, n % HEADS


def slot_of(q, c, j):
    return (q * CHUNKS + c) * HEADS + j


def jobs_at(i, n):
    whole, n = divmod(n, SLOTS)
    i = i + whole if whole else i
    name, off = JOB_AT.get(n, (None, 0))
    return [(name, i, i + off)] if name and (i + off).live() else []


def read_after(name):
    return READ_AFTER.get(name, 1)


def step_at(i, n, after):
    i, q, c, j = moved(i, 0, 0, 0, n - after)
    return [(i, q, c)] if j == 0 and i.live() else []


def turn_of(at, i, n, graph):
    whole, at = divmod(at, SLOTS)
    g = i + (graph - whole)
    return [g] if at == n and g.live() else []


def half_turns(at, i, n, graph):
    return [(g, q) for q in (0, 1) for g in turn_of(at + PHASE * q, i, n, graph)]


def tiles_at(table, i, n):
    found = []
    for tile, at in enumerate(table):
        if at % SLOTS == n:
            start = i + -(at // SLOTS)
            if (start + -2).live():
                found.append((start + -2, start, tile))
    return found


def ahead(i, q, c, j, places):
    i, q, c, h = moved(i, q, c, j, places)
    return (i, q, c), h


def score_bank(step, h):
    n, last = slot_of(step[1], step[2], h), SLOTS - 1
    bank = 1 if n == last else n % SCORES
    back = {0: 4, 1: 2, 2: 4, last: 2}.get(n, SCORES)
    return bank, back


def slot(step, h, plus=0):
    i, q, c = step
    return i.times(STEPS * HEADS, (q * CHUNKS + c) * HEADS + h + plus)


def number(step, plus=0):
    i, q, c = step
    return i.times(STEPS, q * CHUNKS + c + plus)


def build(nc, x, adj, Wq, bq, Wk, bk, Wv, bv, Wo, bo, gamma, beta, W, a, out):
    x_half = x.rearrange("b (h t p) f -> (b h) p t f", h=2, p=P)
    out_half = out.rearrange("b (h t p) f -> (b h) p t f", h=2, p=P)
    adj_tile = adj.rearrange("(t p) j -> t p j", p=P)
    h_kept = nc.dram_tensor("h_kept", (2 * BATCHES, P, TILES, D), F32, kind="Internal").ap()
    x1_kept = nc.dram_tensor("x1_kept", (2 * BATCHES, P, TILES, D), F32, kind="Internal").ap()

    ctx = ExitStack()
    with ctx:

        def sb(name, shape, dt=F32):
            return ctx.enter_context(nc.sbuf_tensor(name, shape, dt))

        def pb(name, shape, dt=F32):
            return ctx.enter_context(nc.psum_tensor(name, shape, dt))

        def sem(name):
            return ctx.enter_context(nc.semaphore(name))

        cap = sb("cap", [P, CHUNKS, N])
        see_t = sb("see_t", [P, CHUNKS, N], BF16)
        see = sb("see", [P, CHUNKS, N], BF16)
        key_stack = sb("key_stack", [P, HEADS, N], F32R)
        query_stack = sb("query_stack", [P, HEADS, N], F32R)
        key_parts = sb("key_parts", [P, 2, HALF], F32R)
        query_parts = sb("query_parts", [P, 2, HALF], F32R)
        value = sb("value", [P, CHUNKS, D])
        probs = sb("probs", [P, 2, HEADS, HALF])
        context = sb("context", [P, CHUNKS, HALF])
        sums = sb("sums", [P, HALF])
        inverse = sb("inverse", [P, TILES, HEADS, CHUNKS])
        gathered = sb("gathered", [P, TILES, D])
        scaled = sb("scaled", [P, TILES, D])
        context_t = sb("context_t", [P, HALF])
        x_in = sb("x_in", [P, 2, TILES, D])
        h_t = sb("h_t", [P, N])
        res = sb("res", [P, TILES, D])
        h1 = sb("h1", [P, TILES, D])
        h1_t = sb("h1_t", [P, N])
        wh = sb("wh", [P, CHUNKS, WIDE])
        near_row = sb("near_row", [P, N])
        to_row = sb("to_row", [P, N])
        peak = sb("peak", [P, CHUNKS])
        row_shift = sb("row_shift", [P, 2, CHUNKS])
        gat_inverse = sb("gat_inverse", [P, TILES])
        ring = sb("ring", [P, RING, HALF])
        w_in = h_t[:, 0:4 * D].rearrange("p (n f) -> p n f", n=4)
        w_t = sb("w_t", [P, 4, D])
        w1 = sb("w1", [P, WIDE])
        a_in = sb("a_in", [P, 2])
        bias_col = sb("bias_col", [P, 3])
        bias_v = sb("bias_v", [P, 1])
        rows = sb("rows", [P, 3, D])
        eye = sb("eye", [P, P])
        eye_b = ring[:, 3, 0:P // 2].bitcast(BF16)
        not_eye = ring[:, 2, 0:P // 2].bitcast(BF16)
        one_of = sb("one_of", [P, CHUNKS, DH])
        ones = sb("ones", [P, DH])
        pick = sb("pick", [P, 1])
        eps = sb("eps", [P, TILES])
        minus_half = sb("minus_half", [P, TILES])
        small = sb("small", [P, 4, TILES * 11])
        norm = {}
        w1_a = w1[:, D:WIDE]
        ends = wh[:, :, D:WIDE]
        for n, s in enumerate(("x0", "x1", "y", "z")):
            norm[s] = (small[:, n, 0:24].rearrange("p (t k) -> p t k", t=TILES),
                       small[:, n, 24:32].rearrange("p (t k) -> p t k", t=TILES),
                       small[:, n, 32:36], small[:, n, 36:40], small[:, n, 40:44])

        score = pb("score", [P, SCORES, HALF])
        ctx_ps = pb("ctx_ps", [P, HALF])
        sum_ps = pb("sum_ps", [P, HALF])
        work = pb("work", [P, 2, HALF])
        gat_ps = pb("gat_ps", [P, HALF])

        def in_tiles(bank):
            return work[:, bank, :].rearrange("p (t f) -> p t f", t=TILES)

        w_loaded = sem("w_loaded")
        rest_loaded = sem("rest_loaded")
        adj_loaded = [sem(f"adj_loaded{t}") for t in range(CHUNKS)]
        x_loaded = sem("x_loaded")
        h_stored = sem("h_stored")
        res_loaded = sem("res_loaded")
        x1_stored = sem("x1_stored")
        x1_loaded = sem("x1_loaded")
        out_stored = sem("out_stored")
        keys_stacked = sem("keys_stacked")
        queries_stacked = sem("queries_stacked")
        consts_made = sem("consts_made")
        consts_step = sem("consts_step")
        adj_cast = [sem(f"adj_cast{p}") for p in (0, 1)]
        see_made = sem("see_made")
        adj_turned = sem("adj_turned")
        turned_read = sem("turned_read")
        masks_step = sem("masks_step")
        edges_made = sem("edges_made")
        masks_made = sem("masks_made")
        see_ready = sem("see_ready")
        w_turned = sem("w_turned")
        w_ready = sem("w_ready")
        passed = sem("passed")
        scores_done = sem("scores_done")
        exp_done = sem("exp_done")
        probs_ready = sem("probs_ready")
        context_done = sem("context_done")
        context_read = sem("context_read")
        sums_done = sem("sums_done")
        sums_read = sem("sums_read")
        work_done = [sem(f"work_done{b}") for b in (0, 1)]
        work_read = [sem(f"work_read{b}") for b in (0, 1)]
        high_ready = sem("high_ready")
        gathered_step = sem("gathered_step")
        res_ready = sem("res_ready")
        gamma_done = sem("gamma_done")
        x1_ready = sem("x1_ready")
        stats_done = {s: sem(f"{s}_stats_done") for s in norm}
        moments_done = {s: sem(f"{s}_moments_done") for s in norm}
        spread_done = {s: sem(f"{s}_spread_done") for s in norm}
        rstd_done = {s: sem(f"{s}_rstd_done") for s in norm}
        shift_done = {s: sem(f"{s}_shift_done") for s in norm}
        normed = {s: sem(f"{s}_normed") for s in norm}
        peak_step = sem("peak_step")
        peak_done = sem("peak_done")
        leaky_done = sem("leaky_done")
        hidden_done = sem("hidden_done")
        hidden_late = sem("hidden_late")
        gat_exp_done = sem("gat_exp_done")
        gat_done = sem("gat_done")
        gat_read = sem("gat_read")
        divided = sem("divided")
        positive_ready = sem("positive_ready")
        negative_ready = sem("negative_ready")
        negative_exp = sem("negative_exp")
        elu_step = sem("elu_step")
        out_ready = sem("out_ready")

        def wait(engine, semaphore, value):
            if not isinstance(value, int) or value > 0:
                engine.wait_ge(semaphore, value)

        def stand_alone(engine):
            engine.sem_inc(passed, 1)

        def adj_raw(t):
            home = context if t < 4 else probs[:, 0] if t < 6 else probs[:, 1]
            at = t if t < 4 else (t - 4) % 2
            return home[:, 2 * at:2 * at + 2, :].rearrange("p a n -> p (a n)").bitcast(I32)

        def bf16_slot(s):
            return ring[:, s, :].bitcast(BF16)

        def adj_bf16(t):
            return bf16_slot(t % 2)

        def turned_bf16(t):
            return bf16_slot(4 + t % 2)

        def edges_bf16(t):
            return bf16_slot(6 + t % 2)

        def adj_turned_ps(t):
            return score[:, t % SCORES, :].bitcast(BF16)

        def second_weights_step(i, n):
            return i.register is None and i.offset == FIRST and n == WEIGHTS_AT

        def mask_step(i, n):
            if i.register is None and i.offset == FIRST and n in MASKS_AT:
                return MASKS_AT.index(n)
            return None

        def ring_tiles(s):
            return ring[:, s, :].rearrange("p (t f) -> p t f", t=TILES)

        def shared(g, n):
            return g.register is None and g.offset >= BATCHES - 2 and n % 2 == 1

        def wait_hidden(engine, g, n):
            late = 0 if g.register is not None else max(0, g.offset - (BATCHES - 2))
            if shared(g, n):
                engine.wait_ge(hidden_late, late * CHUNKS + n // 2 + 1)
            elif g.register is None and g.offset >= BATCHES - 2:
                engine.wait_ge(hidden_done, (BATCHES - 2) * 2 * CHUNKS + late * CHUNKS + n // 2 + 1)
            else:
                engine.wait_ge(hidden_done, g.times(2 * CHUNKS, n + 1))

        block = ctx.enter_context(nc.Block())

        @block.sync
        def _(sp):
            for q in (0, 1):
                sp.dma_start(x_in[:, q], x_half[q]).then_inc(x_loaded, 16)
            sp.wait_ge(x_loaded, 32)
            for t in range(CHUNKS):
                sp.dma_start(adj_raw(t), adj_tile[t]).then_inc(adj_loaded[t], 16)
            sp.dma_start(w1[:, 0:D], W).then_inc(rest_loaded, 16)
            for e in (0, 1):
                sp.dma_start(a_in[:, e:e + 1], a[e * D:(e + 1) * D, :]).then_inc(rest_loaded, 16)
            for n, b in enumerate((bo, gamma, beta)):
                row = b.rearrange("(o f) -> o f", o=1).broadcast_to([P, D])
                sp.dma_start(rows[:, n, :], row).then_inc(rest_loaded, 16)
            def alone(semaphore, value):
                wait(sp, semaphore, value)
                if not isinstance(value, int):
                    stand_alone(sp)

            def stack(to, parts, picks, q, done):
                for s, part in enumerate(picks):
                    sp.dma_start(to[s * DH:(s + 1) * DH, :, q * HALF:(q + 1) * HALF].bitcast(F32),
                                 parts[:, part, :].bitcast(F32)).then_inc(done, 16)

            def half_of(tensor, b, q):
                row = b.times(2, q)
                if isinstance(row, int):
                    return tensor[row]
                return tensor[bass.ds(row, 1)].rearrange("o p t f -> (o p) t f")

            def at(i, n):
                for f, q in half_turns(SYNC_IN_PHASE["load_residual"], i, n, -1):
                    if f.register is not None or f.offset > 0 or q:
                        turned, before = ("turn_hidden1", f + -1) if q == 0 else ("turn_hidden0", f)
                        alone(work_done[bank_of(turned)], count_of(turned, before))
                        alone(x1_stored, f.times(32, 16 * q))
                    alone(h_stored, f.times(32, 16 * (q + 1)))
                    sp.dma_start(res[:, :, :], half_of(h_kept, f, q)).then_inc(res_loaded, 16)
                    sp.dma_start(h1[:, :, :], half_of(x_half, f, q)).then_inc(res_loaded, 16)
                for half in (0, 1):
                    for g in turn_of(SYNC_SECOND[f"load_x1_{half}"], i, n, -2):
                        alone(work_done[bank_of(f"gat_turn{half}")], count_of(f"gat_turn{half}", g))
                        alone(x1_stored, g.times(32, 16 * (half + 1)))
                        sp.dma_start(ring_tiles(TURN), half_of(x1_kept, g, half)).then_inc(x1_loaded, 16)
                for b in turn_of(SYNC_COMING["stack_query1"], i, n, 1):
                    alone(work_read[bank_of("query1")], count_of("query1", b))
                    alone(scores_done, b.times(SLOTS))
                    stack(query_stack, query_parts, (0, 1, 0, 1), 1, queries_stacked)
                for b in turn_of(SYNC_COMING["stack_query0"], i, n, 1):
                    alone(work_read[bank_of("query0")], count_of("query0", b))
                    alone(scores_done, b.times(SLOTS, -PHASE))
                    stack(query_stack, query_parts, (0, 1, 0, 1), 0, queries_stacked)
                for b in turn_of(SYNC_COMING["stack_key0"], i, n, 1):
                    alone(work_read[bank_of("key0")], count_of("key0", b))
                    alone(scores_done, b.times(SLOTS, -PHASE // 2))
                    stack(key_stack, key_parts, (0, 0, 1, 1), 0, keys_stacked)
                for half in (0, 1):
                    for b in turn_of(SYNC_COMING[f"store_h{half}"], i, n, 1):
                        alone(normed[f"x{half}"], b.times(1, 1))
                        sp.dma_start(half_of(h_kept, b, half), x_in[:, half]).then_inc(h_stored, 16)
                for b in turn_of(SYNC_COMING["load_x"], i, n, 1):
                    if b.register is not None or b.offset > 0:
                        alone(work_done[bank_of("turn_x1")], count_of("turn_x1", b + -1))
                        alone(h_stored, b.times(32))
                        for half in (0, 1):
                            sp.dma_start(x_in[:, half], half_of(x_half, b, half)).then_inc(x_loaded, 16)
                for f, q in half_turns(SYNC_IN_PHASE["store_x1"], i, n, -1):
                    alone(x1_ready, f.times(2, q + 1))
                    sp.dma_start(half_of(x1_kept, f, q), res[:, :, :]).then_inc(x1_stored, 16)
                for b in turn_of(SYNC_COMING["stack_key1"], i, n, 1):
                    alone(work_read[bank_of("key1")], count_of("key1", b))
                    alone(scores_done, b.times(SLOTS))
                    stack(key_stack, key_parts, (0, 0, 1, 1), 1, keys_stacked)
                for half in (0, 1):
                    for g in turn_of(SYNC_SECOND[f"store_out{half}"], i, n, -2):
                        alone(out_ready, g.times(2, half + 1))
                        sp.dma_start(half_of(out_half, g, half), ring_tiles(OUT_A)).then_inc(out_stored, 16)

            def iteration(i):
                for n in range(SLOTS):
                    at(i, n)

            iterations(sp, iteration)
            sp.wait_ge(h_stored, 32 * BATCHES)
            sp.wait_ge(x1_stored, 32 * BATCHES)
            sp.wait_ge(out_stored, 32 * BATCHES)

        @block.gpsimd
        def _(pool):
            nc.gpsimd.memset(eye[:, :], 0.0).then_inc(consts_step, 1)
            nc.gpsimd.memset(not_eye[:, :], 1.0).then_inc(consts_step, 1)
            nc.gpsimd.memset(one_of[:, :, :], 0.0).then_inc(consts_step, 1)
            nc.gpsimd.memset(pick[:, :], 0.0).then_inc(consts_step, 1)
            nc.gpsimd.memset(ones[:, :], 1.0).then_inc(consts_made, 1)
            nc.gpsimd.memset(eps[:, :], EPS).then_inc(consts_made, 1)
            nc.gpsimd.memset(minus_half[:, :], -0.5).then_inc(consts_made, 1)
            pool.wait_ge(consts_step, 4)
            nc.gpsimd.affine_select(out=eye[:, :], in_=eye[:, :], compare_op=ALU.not_equal, fill=1.0, base=0,
                                    pattern=[[-1, P]], channel_multiplier=1).then_inc(consts_step, 1)
            nc.gpsimd.affine_select(out=not_eye[:, :], in_=not_eye[:, :], compare_op=ALU.not_equal, fill=0.0,
                                    base=0, pattern=[[-1, P]], channel_multiplier=1).then_inc(consts_made, 1)
            picked = one_of[:, :, :].rearrange("p c d -> p (c d)")[:, 0:CHUNKS * DH:DH + 1]
            nc.gpsimd.memset(picked, 1.0).then_inc(consts_made, 1)
            for g in range(HEADS):
                pool.wait_ge(consts_made, 5 + g)
                nc.gpsimd.memset(pick[g * DH:g * DH + 1, :], 1.0).then_inc(consts_made, 1)
            pool.wait_ge(consts_step, 5)
            pool.wait_ge(consts_made, 9)
            nc.gpsimd.tensor_copy(eye_b[:, :], eye[:, :]).then_inc(consts_made, 1)
            pool.wait_ge(consts_made, 10)

            def rstd(s, n):
                _, moments, spread, scale, _ = norm[s]
                pool.wait_ge(moments_done[s], n)
                nc.gpsimd.tensor_tensor(spread[:, :], moments[:, :, 1], eps[:, :], ALU.add).then_inc(spread_done[s], 1)
                pool.wait_ge(spread_done[s], n)
                nc.gpsimd.tensor_tensor(scale[:, :], spread[:, :], minus_half[:, :], ALU.pow
                                        ).then_inc(rstd_done[s], 1)

            def hide(g, n):
                half, j = n // CHUNKS, n % CHUNKS
                if shared(g, n):
                    return
                pool.wait_ge(leaky_done, g.times(2 * CHUNKS, n + 1))
                nc.gpsimd.tensor_tensor(ring[:, n % RING, :], ring[:, n % RING, :],
                                        see_t[:, j, half * HALF:(half + 1) * HALF], ALU.add).then_inc(hidden_done, 1)

            def add_residual(g, half):
                pool.wait_ge(x1_loaded, g.times(32, 16 * (half + 1)))
                pool.wait_ge(positive_ready, g.times(2, half + 1))
                nc.gpsimd.tensor_tensor(ring[:, OUT_A, :], ring[:, OUT_A, :], ring[:, TURN, :], ALU.add
                                        ).then_inc(elu_step, 1)

            def add_negative(g, half):
                pool.wait_ge(negative_exp, g.times(2, half + 1))
                pool.wait_ge(elu_step, g.times(2, half + 1))
                nc.gpsimd.tensor_tensor(ring[:, OUT_A, :], ring[:, OUT_A, :], ring[:, OUT_B, :], ALU.add
                                        ).then_inc(out_ready, 1)

            def at(i, q, c, j):
                now = slot_of(q, c, j)
                at_phase = now - PHASE * q
                for half in (0, 1):
                    for g in turn_of(ONCE[f"add_residual{half}"], i, now, -2):
                        add_residual(g, half)
                    for g in turn_of(ONCE[f"add_negative{half}"], i, now, -2):
                        add_negative(g, half)
                f = i + -1
                if f.live():
                    if at_phase == IN_PHASE["residual"] and f.register is None and f.offset == 0:
                        pool.wait_ge(rest_loaded, 16 * 6)
                    if at_phase == IN_PHASE["residual"]:
                        pool.wait_ge(res_loaded, f.times(64, 32 * (q + 1)))
                        nc.gpsimd.tensor_tensor(res[:, :, :], res[:, :, :],
                                                rows[:, 0:1, :].broadcast_to([P, TILES, D]), ALU.add
                                                ).then_inc(res_ready, 1)
                    if at_phase == IN_PHASE["beta"]:
                        nc.gpsimd.tensor_tensor(h1[:, :, :], h1[:, :, :],
                                                rows[:, 2:3, :].broadcast_to([P, TILES, D]), ALU.add
                                                ).then_inc(res_ready, 1)
                    if at_phase == IN_PHASE["rstd_y"]:
                        rstd("y", f.times(2, q + 1))
                    if at_phase == IN_PHASE["gamma"]:
                        pool.wait_ge(normed["y"], f.times(2, q + 1))
                        nc.gpsimd.tensor_tensor(res[:, :, :], res[:, :, :],
                                                rows[:, 1:2, :].broadcast_to([P, TILES, D]), ALU.mult
                                                ).then_inc(gamma_done, 1)
                    if at_phase == IN_PHASE["x1"]:
                        pool.wait_ge(gamma_done, f.times(2, q + 1))
                        pool.wait_ge(res_ready, f.times(4, 2 * q + 2))
                        nc.gpsimd.tensor_tensor(res[:, :, :], res[:, :, :], h1[:, :, :], ALU.add
                                                ).then_inc(x1_ready, 1)
                    if at_phase == IN_PHASE["rstd_z"]:
                        rstd("z", f.times(2, q + 1))
                if (i + 1).live():
                    for x in ("x0", "x1"):
                        if now == ONCE["rstd_" + x]:
                            rstd(x, (i + 1).times(1, 1))
                for name, at_job, _ in jobs_at(i, now - ADD_AFTER):
                    if name.startswith("gather") and name[-1] != "0":
                        pool.wait_ge(work_read[bank_of(name)], count(name, at_job))
                        nc.gpsimd.tensor_tensor(gathered[:, :, :], gathered[:, :, :], scaled[:, :, :], ALU.add
                                                ).then_inc(gathered_step, 1)
                for g, _, n in tiles_at(HIDE_AT, i, now):
                    if n == 0 and g.register is None and g.offset == 0:
                        pool.wait_ge(see_ready, 2 * CHUNKS)
                    hide(g, n)
                if mask_step(i, now) == CHUNKS:
                    pool.wait_ge(masks_made, CHUNKS)
                    pool.wait_ge(see_made, CHUNKS)
                    for t in range(CHUNKS):
                        for m in (see, see_t):
                            spot = m[:, t, t * P:(t + 1) * P]
                            nc.gpsimd.tensor_tensor(spot, spot, not_eye[:, :], ALU.mult).then_inc(see_ready, 1)

            def iteration(i):
                for q in (0, 1):
                    for c in range(CHUNKS):
                        for j in range(HEADS):
                            at(i, q, c, j)

            iterations(pool, iteration)

        @block.scalar
        def _(act):
            for n, w in enumerate((Wq, Wk, Wv, Wo)):
                act.dma_start(w_in[:, n, :], w).then_inc(w_loaded, 16)
            for n, b in enumerate((bq, bk)):
                act.dma_start(bias_col[:, n:n + 1], b.rearrange("(h d o) -> d h o", h=HEADS, o=1),
                              allow_slow_non_contiguous=True).then_inc(w_loaded, 16)
            act.dma_start(bias_col[:, 2:3], bv.rearrange("(f o) -> f o", o=1)).then_inc(w_loaded, 16)
            def second_weights():
                act.wait_ge(w_turned, 2)
                nc.scalar.copy(h1_t[:, 0:D], gat_ps[:, 0:D]).then_inc(w_ready, 1)
                act.wait_ge(w_turned, 3)
                nc.scalar.copy(w1_a[:, 0:2], sum_ps[:, 0:2]).then_inc(w_ready, 1)
                nc.scalar.mul(w1_a[:, 2:3], sum_ps[:, 1:2], 1 - SLOPE).then_inc(w_ready, 1)
                nc.scalar.mul(w1_a[:, 3:4], sum_ps[:, 1:2], SLOPE).then_inc(w_ready, 1)

            def first_weights():
                act.wait_ge(w_turned, 1)
                turned = ctx_ps[:, :].rearrange("p (t f) -> p t f", t=4)
                nc.scalar.copy(w_t[:, 2:4, :], turned[:, 2:4, :])
                nc.scalar.copy(w_t[:, 0:2, :].rearrange("p n (d h) -> p n h d", h=HEADS),
                               turned[:, 0:2, :].rearrange("p n (h d) -> p n h d", h=HEADS)).then_inc(w_ready, 1)
                act.wait_ge(w_loaded, 16 * 7)
                nc.scalar.mul(bias_v[:, :], bias_col[:, 2:3], float(CHUNKS)).then_inc(w_ready, 1)
                act.wait_ge(w_ready, 2)

            def apply(s, n, to, source, function):
                _, _, _, scale, shift = norm[s]
                act.wait_ge(shift_done[s], n)
                for t in range(TILES):
                    last = nc.scalar.activation(to[:, t, :], source[:, t, :], function, bias=shift[:, t:t + 1],
                                                scale=scale[:, t:t + 1])
                last.then_inc(normed[s], 1)

            def gat_exp(g, n):
                wait_hidden(act, g, n)
                nc.scalar.activation(ring[:, n % RING, :], ring[:, n % RING, :], ACT.Exp,
                                     bias=ends[:, n % CHUNKS, 3:4]).then_inc(gat_exp_done, 1)

            def read_gat(g, half):
                act.wait_ge(gat_done, g.times(2, half + 1))
                act.wait_ge(work_done[bank_of(f"gat_sums{half}")], count_of(f"gat_sums{half}", g))
                wait(act, out_ready, g.times(2, half))
                nc.scalar.copy(ring[:, TURN, :], gat_ps[:, :]).then_inc(gat_read, 1)

            def negative_part(g, half):
                act.wait_ge(negative_ready, g.times(2, half + 1))
                nc.scalar.activation(ring[:, OUT_B, :], ring[:, OUT_B, :], ACT.Exp).then_inc(negative_exp, 1)

            def read_job(name, i, b):
                bank = bank_of(name)
                half = int(name[-1])
                side = slice(half * HALF, (half + 1) * HALF)
                act.wait_ge(work_done[bank], count(name, i))
                if name.startswith("query") or name.startswith("key"):
                    is_key = name.startswith("key")
                    parts = key_parts if is_key else query_parts
                    wait(act, keys_stacked if is_key else queries_stacked, b.times(128, 64 * half))
                    nc.scalar.activation(parts[:, 0, :], work[:, bank, :], ACT.Identity,
                                         bias=bias_col[:, int(is_key):int(is_key) + 1]).then_inc(high_ready, 1)
                    return
                if name.startswith("turn_context"):
                    nc.scalar.activation(context_t[:, :], work[:, bank, :], ACT.Identity, bias=bias_v[:, :]
                                         ).then_inc(work_read[bank], 1)
                    return
                if name.startswith("value"):
                    to = value[:, half * TILES:(half + 1) * TILES, :].rearrange("p t f -> p (t f)")
                elif name.startswith("turn_hidden"):
                    to = h1_t[:, side]
                elif name.startswith("turn_x"):
                    to = h_t[:, side]
                elif name.startswith("wh"):
                    wait(act, leaky_done, b.times(2 * CHUNKS))
                    tiles = WH_TILES[name]
                    nc.scalar.copy(wh[:, tiles[0]:tiles[-1] + 1, :].rearrange("p t f -> p (t f)"),
                                   work[:, bank, 0:len(tiles) * WIDE]).then_inc(work_read[bank], 1)
                    return
                elif name.startswith("to_row"):
                    wait(act, leaky_done, b.times(2 * CHUNKS))
                    to = to_row[:, side]
                elif name.startswith("base_row"):
                    to = to_row[:, side]
                elif name.startswith("near_row"):
                    to = near_row[:, side]
                else:
                    assert name.startswith("gat_sums"), name
                    to = ring[:, SUMS, :]
                nc.scalar.copy(to, work[:, bank, :]).then_inc(work_read[bank], 1)

            def at(i, q, c, j):
                if second_weights_step(i, slot_of(q, c, j)):
                    second_weights()
                t = mask_step(i, slot_of(q, c, j))
                if t is not None and t < CHUNKS and t % 2 == 0:
                    act.wait_ge(adj_loaded[t], 16)
                    if t >= 2:
                        act.wait_ge(adj_turned, t - 1)
                        act.wait_ge(see_made, t - 1)
                    nc.scalar.copy(adj_bf16(t), adj_raw(t)).then_inc(adj_cast[0], 1)
                if t:
                    act.wait_ge(adj_turned, t)
                    if t >= 3:
                        act.wait_ge(edges_made, t - 2)
                    nc.scalar.copy(turned_bf16(t - 1), adj_turned_ps(t - 1)).then_inc(turned_read, 1)
                step, h = ahead(i, q, c, j, EXP_AHEAD)
                if step[0].live():
                    bank, _ = score_bank(step, h)
                    act.wait_ge(scores_done, slot(step, h, 1))
                    nc.scalar.activation(score[:, bank, :], score[:, bank, :], ACT.Exp, scale=DH ** -0.5
                                         ).then_inc(exp_done, 1)
                now = slot_of(q, c, j)
                for step in step_at(i, now, CONTEXT_READ_AT):
                    i_step, q_step, chunk = step
                    act.wait_ge(context_done, number(step, 1))
                    if (i_step + (q_step - 1)).live():
                        turned = f"gather{q_step}{chunk}"
                        act.wait_ge(work_done[bank_of(turned)], count_of(turned, i_step + (q_step - 1)))
                    nc.scalar.copy(context[:, chunk, :], ctx_ps[:, :]).then_inc(context_read, 1)
                for step in step_at(i, now, SUMS_READ_AT):
                    if step[2] == CHUNKS - 1:
                        act.wait_ge(sums_done, number(step, 1))
                        nc.scalar.copy(sums[:, :], sum_ps[:, :]).then_inc(sums_read, 1)
                at_phase = now - PHASE * q
                for back in (3, 2, 1):
                    for name, at_job, b in jobs_at(i, now - back):
                        after = HIGH_AFTER if name.startswith(("query", "key")) else read_after(name)
                        if not name.startswith(READ_BY_VECTOR) and after == back:
                            read_job(name, at_job, b)
                f = i + -1
                if f.live():
                    n = f.times(2, q + 1)
                    if at_phase == IN_PHASE["apply_y"]:
                        apply("y", n, res, res, ACT.Identity)
                    if at_phase == IN_PHASE["apply_z"]:
                        apply("z", n, h1, res, ACT.Relu)
                if (i + 1).live():
                    for half in (0, 1):
                        if now == ONCE[f"apply_x{half}"]:
                            apply(f"x{half}", (i + 1).times(1, 1), x_in[:, half], x_in[:, half], ACT.Relu)
                            if half == 1 and i.register is None and i.offset == FIRST:
                                first_weights()
                for g, _, n in tiles_at(GAT_EXP_AT, i, now):
                    gat_exp(g, n)
                for half in (0, 1):
                    for g in turn_of(ONCE[f"read_gat{half}"], i, now, -2):
                        read_gat(g, half)
                    for g in turn_of(ONCE[f"negative{half}"], i, now, -2):
                        negative_part(g, half)

            def iteration(i):
                for q in (0, 1):
                    for c in range(CHUNKS):
                        for j in range(HEADS):
                            at(i, q, c, j)

            iterations(act, iteration)

        @block.vector
        def _(dve):

            def masks(t):
                if t < CHUNKS and t % 2 == 1:
                    dve.wait_ge(adj_loaded[t], 16)
                    if t >= 2:
                        dve.wait_ge(adj_turned, t - 1)
                    nc.vector.tensor_copy(adj_bf16(t), adj_raw(t)).then_inc(adj_cast[1], 1)
                if t < CHUNKS:
                    dve.wait_ge(adj_cast[t % 2], t // 2 + 1)
                    nc.vector.tensor_scalar(see[:, t, :], adj_bf16(t), 0.0, OUT_OF_SIGHT, ALU.is_le, ALU.mult
                                            ).then_inc(see_made, 1)
                if t:
                    dve.wait_ge(turned_read, t)
                    nc.vector.tensor_scalar(edges_bf16(t - 1), turned_bf16(t - 1), 0.0, None, ALU.not_equal
                                            ).then_inc(masks_step, 1)
                    columns = slice((t - 1) * P, t * P)
                    nc.vector.tensor_scalar(see_t[:, :, columns],
                                            turned_bf16(t - 1).rearrange("p (j i) -> p j i", i=P), 0.0,
                                            OUT_OF_SIGHT, ALU.is_le, ALU.mult).then_inc(edges_made, 1)
                    dve.wait_ge(masks_step, t)
                    nc.vector.tensor_scalar(cap[:, :, columns],
                                            edges_bf16(t - 1).rearrange("p (j i) -> p j i", i=P), HIGH, LOW,
                                            ALU.mult, ALU.max).then_inc(masks_made, 1)

            def moments(s, n, source):
                stats, moment, _, _, _ = norm[s]
                for t in range(TILES):
                    last = nc.vector.bn_stats(stats[:, t, :], source[:, t, :])
                last.then_inc(stats_done[s], 1)
                dve.wait_ge(stats_done[s], n)
                stand_alone(dve)
                for t in range(TILES):
                    last = nc.vector.bn_aggr(moment[:, t, :], stats[:, t, :])
                last.then_inc(moments_done[s], 1)

            def shift(s, n):
                _, moment, _, scale, to = norm[s]
                dve.wait_ge(rstd_done[s], n)
                nc.vector.scalar_tensor_tensor(out=to[:, :], in0=moment[:, :, 0], scalar=-1.0, in1=scale[:, :],
                                               op0=ALU.mult, op1=ALU.mult).then_inc(shift_done[s], 1)

            def heads(tile):
                return tile.rearrange("p t (h d) -> p t h d", h=HEADS)

            def gather(i, name, b, q, chunk):
                to = gathered if chunk == 0 else scaled
                if chunk == 0:
                    sums_job = f"turn_sums{1 - q}"
                    dve.wait_ge(work_read[bank_of(sums_job)], count_of(sums_job, b))
                wait(dve, gathered_step, b.times(14, 7 * q + max(chunk - 1, 0)))
                dve.wait_ge(work_done[bank_of(name)], count(name, i))
                share = inverse[:, :, :, chunk:chunk + 1].broadcast_to([P, TILES, HEADS, DH])
                nc.vector.tensor_tensor(heads(to[:, :, :]), heads(in_tiles(bank_of(name))), share, ALU.mult
                                        ).then_inc(work_read[bank_of(name)], 1)

            def see_peak(g, t):
                if t:
                    dve.wait_ge(peak_step, g.times(PEAK_STEPS, t))
                    stand_alone(dve)
                nc.vector.tensor_tensor_reduce(
                    out=ring[:, OUT_A:OUT_B + 1, :].rearrange("p a n -> p (a n)"), in0=to_row[:, :], in1=see[:, t, :],
                    scale=1.0, scalar=-3e38, op0=ALU.add, op1=ALU.max, accum_out=peak[:, t:t + 1]
                ).then_inc(peak_step, 1)

            def shifts(g):
                dve.wait_ge(peak_step, g.times(PEAK_STEPS, CHUNKS))
                nc.vector.tensor_tensor(peak[:, :], peak[:, :], ends[:, :, 0], ALU.add).then_inc(peak_step, 1)
                dve.wait_ge(peak_step, g.times(PEAK_STEPS, CHUNKS + 1))
                nc.vector.scalar_tensor_tensor(out=peak[:, :], in0=peak[:, :], scalar=SLOPE, in1=peak[:, :],
                                               op0=ALU.mult, op1=ALU.max).then_inc(peak_step, 1)
                dve.wait_ge(peak_step, g.times(PEAK_STEPS, CHUNKS + 2))
                for n, part in enumerate((1.0, SLOPE)):
                    nc.vector.scalar_tensor_tensor(out=row_shift[:, n, :], in0=ends[:, :, 0], scalar=part,
                                                   in1=peak[:, :], op0=ALU.mult, op1=ALU.subtract).then_inc(peak_done, 1)

            def leaky(g, n, i):
                half, j = n // CHUNKS, n % CHUNKS
                if n % CHUNKS == 0:
                    for name in (f"near_row{half}", f"base_row{half}"):
                        dve.wait_ge(work_read[bank_of(name)], count_of(name, g))
                if n == TURN:
                    wait(dve, out_stored, g.times(32))
                if n == RING:
                    dve.wait_ge(work_done[bank_of("gat_sums0")], count_of("gat_sums0", g))
                side = slice(half * HALF, (half + 1) * HALF)
                nc.vector.scalar_tensor_tensor(out=ring[:, n % RING, :], in0=near_row[:, side],
                                               scalar=ends[:, j, 2:3], in1=to_row[:, side],
                                               op0=ALU.add, op1=ALU.max).then_inc(leaky_done, 1)
                if shared(g, n):
                    dve.wait_ge(leaky_done, g.times(2 * CHUNKS, n + 1))
                    nc.vector.tensor_tensor(ring[:, n % RING, :], ring[:, n % RING, :], see_t[:, j, side], ALU.add
                                            ).then_inc(hidden_late, 1)

            def divide_gat(i, g, half):
                name = f"gat_turn{half}"
                bank = bank_of(name)
                sums_job = f"gat_turn_sums{half}"
                dve.wait_ge(work_read[bank_of(sums_job)], count_of(sums_job, g))
                dve.wait_ge(work_done[bank], count(name, i))
                wait(dve, out_stored, g.times(32, 16 * half))
                nc.vector.tensor_tensor(ring_tiles(OUT_A), in_tiles(bank),
                                        gat_inverse[:, :].unsqueeze(2).broadcast_to([P, TILES, D]), ALU.mult
                                        ).then_inc(work_read[bank], 1)
                dve.wait_ge(work_read[bank], count(name, i))
                nc.vector.tensor_scalar(ring[:, OUT_B, :], ring[:, OUT_A, :], 0.0, None, ALU.min
                                        ).then_inc(negative_ready, 1)
                nc.vector.tensor_scalar(ring[:, OUT_A, :], ring[:, OUT_A, :], 0.0, -1.0, ALU.max, ALU.add
                                        ).then_inc(positive_ready, 1)

            def read_job(name, i, b):
                bank = bank_of(name)
                digits = [int(d) for d in name if d.isdigit()]
                if name.startswith("query") or name.startswith("key"):
                    is_key = name.startswith("key")
                    parts = key_parts if is_key else query_parts
                    turn = {"query0": 1, "key0": 2, "key1": 3, "query1": 4}[name]
                    dve.wait_ge(high_ready, b.times(4, turn))
                    nc.vector.scalar_tensor_tensor(
                        out=parts[:, 1, :], in0=work[:, bank, :], scalar=bias_col[:, int(is_key):int(is_key) + 1],
                        in1=parts[:, 0, :].bitcast(F32), op0=ALU.add, op1=ALU.subtract
                    ).then_inc(work_read[bank], 1)
                    return
                if name.startswith("gather"):
                    gather(i, name, b, 1 - digits[0], digits[1])
                    return
                if name.startswith("gat_turn") and not name.startswith("gat_turn_sums"):
                    divide_gat(i, b, digits[0])
                    return
                dve.wait_ge(work_done[bank], count(name, i))
                if name.startswith("turn_sums"):
                    found = work[:, bank, :].rearrange("p (t h r) -> p t h r", t=TILES, h=HEADS)
                    nc.vector.reciprocal(inverse[:, :, :, :], found[:, :, :, 0:CHUNKS]).then_inc(work_read[bank], 1)
                elif name.startswith("project"):
                    q = digits[0]
                    dve.wait_ge(res_ready, b.times(4, 2 * q + 1))
                    nc.vector.tensor_tensor(res[:, :, :], in_tiles(bank), res[:, :, :], ALU.add
                                            ).then_inc(work_read[bank], 1)
                    dve.wait_ge(work_read[bank], count(name, i))
                    moments("y", b.times(2, q + 1), res)
                else:
                    assert name.startswith("gat_turn_sums"), name
                    nc.vector.reciprocal(gat_inverse[:, :], work[:, bank, 0:TILES]).then_inc(work_read[bank], 1)

            def at(i, q, c, j):
                t = mask_step(i, slot_of(q, c, j))
                if t is not None:
                    masks(t)
                step, h = ahead(i, q, c, j, PROBS_AHEAD)
                if step[0].live():
                    if h == 0:
                        wait(dve, sums_done, number(step, -1))
                        if step[0].register is None and step[0].offset == 0 and step[1:] == (0, 0):
                            dve.wait_ge(masks_made, CHUNKS)
                    dve.wait_ge(exp_done, slot(step, h, 1))
                    nc.vector.scalar_tensor_tensor(
                        out=probs[:, step[2] % 2, h, :], in0=score[:, score_bank(step, h)[0], :], scalar=LOW,
                        in1=cap[:, step[2], step[1] * HALF:(step[1] + 1) * HALF],
                        op0=ALU.max, op1=ALU.min).then_inc(probs_ready, 1)
                now = slot_of(q, c, j)
                at_phase = now - PHASE * q
                for back in (3, 2, 1):
                    for name, at_job, b in jobs_at(i, now - back):
                        if name.startswith(READ_BY_VECTOR + ("query", "key")) and read_after(name) == back:
                            read_job(name, at_job, b)
                f = i + -1
                if f.live():
                    n = f.times(2, q + 1)
                    if at_phase == IN_PHASE["shift_y"]:
                        shift("y", n)
                    if at_phase == IN_PHASE["moments_z"]:
                        dve.wait_ge(x1_ready, n)
                        moments("z", n, res)
                    if at_phase == IN_PHASE["shift_z"]:
                        shift("z", n)
                if (i + 1).live():
                    n = (i + 1).times(1, 1)
                    for half in (0, 1):
                        if now == ONCE[f"moments_x{half}"]:
                            dve.wait_ge(x_loaded, (i + 1).times(32, 32))
                            moments(f"x{half}", n, x_in[:, half])
                        if now == ONCE[f"shift_x{half}"]:
                            shift(f"x{half}", n)
                for g, start, t in tiles_at(PEAKS_AT, i, now):
                    if t == 0:
                        wait(dve, out_stored, g.times(32, -16))
                        if g.register is None and g.offset == 0:
                            dve.wait_ge(see_ready, 2 * CHUNKS)
                        dve.wait_ge(work_read[bank_of("to_row1")], count_of("to_row1", g))
                        stand_alone(dve)
                    see_peak(g, t)
                    if t == CHUNKS - 1:
                        for name in WH_TILES:
                            dve.wait_ge(work_read[bank_of(name)], count_of(name, g))
                        shifts(g)
                for g, start, n in tiles_at(LEAKY_AT, i, now):
                    leaky(g, n, start)
            def iteration(i):
                for q in (0, 1):
                    for c in range(CHUNKS):
                        for j in range(HEADS):
                            at(i, q, c, j)

            iterations(dve, iteration)

        @block.tensor
        def _(pe):
            pe.wait_ge(w_loaded, 16 * 7)
            pe.wait_ge(consts_made, 10)
            for n in range(4):
                last = nc.tensor.transpose(ctx_ps[:, n * D:(n + 1) * D], w_in[:, n, :], eye[:, :])
            last.then_inc(w_turned, 1)

            def second_weights():
                pe.wait_ge(rest_loaded, 16 * 6)
                nc.tensor.transpose(gat_ps[:, 0:D], w1[:, 0:D], eye[:, :]).then_inc(w_turned, 1)
                pe.wait_ge(w_ready, 3)
                nc.tensor.matmul(sum_ps[:, 0:2], h1_t[:, 0:D], a_in[:, :], start=True, stop=True
                                 ).then_inc(w_turned, 1)
                pe.wait_ge(w_ready, 6)

            def turn(bank, source):
                for t in range(TILES):
                    last = nc.tensor.transpose(work[:, bank, t * P:(t + 1) * P], source(t), eye[:, :])
                return last

            def product(bank, pairs):
                for t, (left, right) in enumerate(pairs):
                    last = nc.tensor.matmul(work[:, bank, t * P:(t + 1) * P], left, right, start=True, stop=True)
                return last

            def wait_read(name, graph):
                wait(pe, work_read[bank_of(name)], count_of(name, graph))

            def job(i, name, b):
                bank = bank_of(name)
                wait(pe, work_read[bank], count(name, i) + -1)
                half = int(name[-1]) if name[-1].isdigit() else 0
                side = slice(half * HALF, (half + 1) * HALF)
                if name.startswith("gather"):
                    chunk = int(name[-1])
                    pe.wait_ge(context_read, number((b, 1 - int(name[6]), chunk), 1))
                    last = turn(bank, lambda t: context[:, chunk, t * P:(t + 1) * P])
                elif name.startswith("turn_sums"):
                    pe.wait_ge(sums_read, b.times(2, (1 - half) + 1))
                    last = turn(bank, lambda t: sums[:, t * P:(t + 1) * P])
                elif name.startswith("turn_context"):
                    pe.wait_ge(gathered_step, b.times(14, 7 * (half + 1)))
                    last = turn(bank, lambda t: gathered[:, t, :])
                elif name.startswith("project"):
                    wait_read(f"turn_context{half}", b)
                    last = product(bank, [(context_t[:, t * P:(t + 1) * P], w_t[:, 3, :]) for t in range(TILES)])
                elif name.startswith("turn_hidden"):
                    pe.wait_ge(normed["z"], b.times(2, half + 1))
                    last = turn(bank, lambda t: h1[:, t, :])
                elif name.startswith("turn_x"):
                    pe.wait_ge(normed[f"x{half}"], b.times(1, 1))
                    last = turn(bank, lambda t: x_in[:, half, t, :])
                elif name.startswith("query"):
                    if half == 0:
                        wait_read("turn_x1", b)
                        if b.register is None and b.offset == 0:
                            pe.wait_ge(w_ready, 1)
                    last = nc.tensor.matmul(work[:, bank, :], w_t[:, 0, :], h_t[:, side], start=True, stop=True)
                elif name.startswith("key"):
                    last = nc.tensor.matmul(work[:, bank, :], w_t[:, 1, :], h_t[:, side], start=True, stop=True)
                elif name.startswith("value"):
                    last = product(bank, [(h_t[:, (half * TILES + t) * P:(half * TILES + t + 1) * P], w_t[:, 2, :])
                                    for t in range(TILES)])
                elif name.startswith("wh"):
                    for n, t in enumerate(WH_TILES[name]):
                        last = nc.tensor.matmul(work[:, bank, n * WIDE:(n + 1) * WIDE], h1_t[:, t * P:(t + 1) * P],
                                                w1[:, :], start=True, stop=True)
                elif name.startswith("to_row"):
                    if half == 0:
                        wait_read("turn_hidden1", b)
                    last = nc.tensor.matmul(work[:, bank, :], w1_a[:, 1:2].broadcast_to([P, P]), h1_t[:, side],
                                            start=True, stop=True)
                elif name.startswith("near_row") or name.startswith("base_row"):
                    pe.wait_ge(peak_done, b.times(2, 2))
                    kind = int(name.startswith("base"))
                    last = product(bank, [(row_shift[:, kind, half * TILES + t:half * TILES + t + 1].broadcast_to([P, P]),
                                     eye[:, :]) for t in range(TILES)])
                elif name.startswith("gat_sums"):
                    pe.wait_ge(gat_exp_done, b.times(2 * CHUNKS, CHUNKS * (half + 1)))
                    for jt in range(CHUNKS):
                        g = jt % 4
                        last = nc.tensor.matmul(work[g * DH:(g + 1) * DH, bank, :], ones[:, :],
                                                ring[:, (half * CHUNKS + jt) % RING, :],
                                                start=jt < 4, stop=jt >= 4)
                elif name.startswith("gat_turn_sums"):
                    wait_read(f"gat_sums{half}", b)
                    for t in range(TILES):
                        last = nc.tensor.matmul(work[:, bank, t:t + 1], ring[:, SUMS, t * P:(t + 1) * P], pick[:, :],
                                                start=True, stop=True)
                else:
                    assert name.startswith("gat_turn"), name
                    pe.wait_ge(gat_read, b.times(2, half + 1))
                    last = turn(bank, lambda t: ring[:, TURN, t * P:(t + 1) * P])
                last.then_inc(work_done[bank], 1)

            def neighbours(g, n):
                half, jt = n // CHUNKS, n % CHUNKS
                pe.wait_ge(gat_exp_done, g.times(2 * CHUNKS, n + 1))
                if jt == 0:
                    wait(pe, gat_read, g.times(2, half))
                last = nc.tensor.matmul(gat_ps[:, :], wh[:, jt, 0:D], ring[:, n % RING, :], start=jt == 0,
                                        stop=jt == CHUNKS - 1)
                if jt == CHUNKS - 1:
                    last.then_inc(gat_done, 1)

            def at(i, q, c, j):
                if second_weights_step(i, slot_of(q, c, j)):
                    second_weights()
                t = mask_step(i, slot_of(q, c, j))
                if t is not None and t < CHUNKS:
                    pe.wait_ge(adj_cast[t % 2], t // 2 + 1)
                    if t >= SCORES:
                        pe.wait_ge(turned_read, t - SCORES + 1)
                    for jt in range(CHUNKS):
                        last = nc.tensor.transpose(adj_turned_ps(t)[:, jt * P:(jt + 1) * P],
                                                   adj_bf16(t)[:, jt * P:(jt + 1) * P], eye_b[:, :])
                    last.then_inc(adj_turned, 1)
                step, h = ahead(i, q, c, j, SCORES_AHEAD)
                if step[0].live():
                    b, sq, sc = step
                    if h == 0 and sc == 0:
                        pe.wait_ge(queries_stacked, b.times(128, 64 * (sq + 1)))
                    if h == 0 and sq == 0 and sc in (0, TILES):
                        pe.wait_ge(keys_stacked, b.times(128, 64 * (sc // TILES + 1)))
                    if b.register is None and b.offset == 0 and (sq, sc, h) == (0, 0, 0):
                        pe.wait_ge(turned_read, CHUNKS)
                    bank, back = score_bank(step, h)
                    wait(pe, probs_ready, slot(step, h, 1 - back))
                    nc.tensor.matmul(score[:, bank, :], key_stack[:, h, sc * P:(sc + 1) * P],
                                     query_stack[:, h, sq * HALF:(sq + 1) * HALF], start=True, stop=True
                                     ).then_inc(scores_done, 1)
                now = slot_of(q, c, j)
                for step in step_at(i, now, CONTEXT_AT):
                    graph, half, chunk = step
                    if (half, chunk) == (0, 0):
                        wait_read("value0", graph)
                    if (half, chunk) == (0, TILES):
                        wait_read("value1", graph)
                    pe.wait_ge(probs_ready, slot(step, HEADS))
                    wait(pe, context_read, number(step))
                    for h in range(HEADS):
                        last = nc.tensor.matmul(ctx_ps[h * DH:(h + 1) * DH, :], value[:, chunk, h * DH:(h + 1) * DH],
                                                probs[:, chunk % 2, h, :], start=True, stop=True)
                    last.then_inc(context_done, 1)
                for step in step_at(i, now, SUMS_AT):
                    graph, half, chunk = step
                    pe.wait_ge(probs_ready, slot(step, HEADS))
                    if chunk == 0:
                        wait(pe, sums_read, graph.times(2, half))
                    for h in range(HEADS):
                        last = nc.tensor.matmul(sum_ps[h * DH:(h + 1) * DH, :], one_of[:, chunk, :],
                                                probs[:, chunk % 2, h, :], start=chunk == 0,
                                                stop=chunk == CHUNKS - 1)
                    last.then_inc(sums_done, 1)
                for name, at_job, b in jobs_at(i, now):
                    job(at_job, name, b)
                for g, _, n in tiles_at(NEIGHBOURS_AT, i, now):
                    neighbours(g, n)

            def iteration(i):
                for q in (0, 1):
                    for c in range(CHUNKS):
                        for j in range(HEADS):
                            at(i, q, c, j)

            iterations(pe, iteration)


_INS = ["x", "adj", "L0_gnn_Wq", "L0_gnn_bq", "L0_gnn_Wk", "L0_gnn_bk", "L0_gnn_Wv", "L0_gnn_bv", "L0_gnn_Wo",
        "L0_gnn_bo", "L0_gnn_gamma", "L0_gnn_beta", "L1_gnn_W", "L1_gnn_a"]


def kernel(**inputs):
    import numpy as np
    import concourse.bacc as bacc
    from concourse.bass_utils import run_bass_kernel_spmd

    nc = bacc.Bacc("TRN2", target_bir_lowering=False, num_devices=1)
    arrays, args = {}, []
    for name in _INS:
        array = np.ascontiguousarray(inputs[name])
        arrays[f"in_{name}"] = array
        args.append(nc.dram_tensor(f"in_{name}", array.shape, mybir.dt.from_np(array.dtype), kind="ExternalInput").ap())
    args.append(nc.dram_tensor("out_0", (BATCHES, N, D), F32, kind="ExternalOutput").ap())
    build(nc, *args)
    result = run_bass_kernel_spmd(nc, [arrays], core_ids=[0])
    return result.results[0]["out_0"]
```
